# Optimizing a Trainium2 kernel written in Bass

```python
import numpy as np
import jax
import jax.numpy as jnp

def _softmax(x, axis=-1):
    return jax.nn.softmax(x, axis=axis)

def _gelu(x):
    return jax.nn.gelu(x, approximate=True)

def _silu(x):
    return jax.nn.silu(x)

def _sigmoid(x):
    return jax.nn.sigmoid(x)

def _layernorm(x, axis=-1, eps=1e-05):
    m = jnp.mean(x, axis=axis, keepdims=True)
    v = jnp.var(x, axis=axis, keepdims=True)
    return (x - m) / jnp.sqrt(v + eps)

def _scatter_add(tgt, idx, src, axis=0):
    return tgt.at[idx].add(src)

def _segment_sum(src, seg, n):
    return jax.ops.segment_sum(src, seg, n)
kernel_name = 'mk_gnn_preln_d4_gnn_r8_6fb394'

def setup_inputs(seed: int=0):
    np.random.seed(seed)
    _w = jnp.asarray

    def _rec_inputs():
        import jax
        import jax.numpy as jnp
        _gk = jax.random.key(seed)
        x = -0.0001006 + 1 * jax.random.normal(jax.random.fold_in(_gk, 1), (6250, 96), jnp.float32)
        src = jax.random.randint(jax.random.fold_in(_gk, 2), (200000,), 0, 6250, jnp.int32)
        dst = jax.random.randint(jax.random.fold_in(_gk, 3), (200000,), 0, 6250, jnp.int32)
        _o = jnp.argsort(dst, stable=True)
        src = src[_o]
        dst = dst[_o]
        edge_attr_32 = 0.000196303 + 1.00016 * jax.random.normal(jax.random.fold_in(_gk, 12), (200000, 32), jnp.float32)
        return (x, src, dst, edge_attr_32)
    x, src, dst, edge_attr_32 = _rec_inputs()

    def _L0_gnn_setup():
        import jax, jax.numpy as jnp
        import numpy as np
        N_NODES = 6250
        N_EDGES = 100000
        D_IN = 96
        D_HID = 96
        D_OUT = 96

        def _sage_layer(h, src, dst, W_l, b_l, W_r):
            msgs = h[src]
            agg = jax.ops.segment_sum(msgs, dst, num_segments=N_NODES)
            cnt = jax.ops.segment_sum(jnp.ones((src.shape[0], 1), h.dtype), dst, num_segments=N_NODES)
            mean = agg / jnp.maximum(cnt, 1.0)
            return mean @ W_l + b_l + h @ W_r
        key = jax.random.key(seed)
        ks = jax.random.split(key, 8)
        x = jax.random.normal(ks[0], (N_NODES, D_IN), dtype=jnp.float32)
        edge_index = jax.random.randint(ks[1], (2, N_EDGES), 0, N_NODES, dtype=jnp.int32)
        s = 1.0 / np.sqrt(D_IN)
        W1_l = jax.random.uniform(ks[2], (D_IN, D_HID), jnp.float32, -s, s)
        W1_r = jax.random.uniform(ks[3], (D_IN, D_HID), jnp.float32, -s, s)
        b1 = jnp.zeros((D_HID,), jnp.float32)
        s2 = 1.0 / np.sqrt(D_HID)
        W2_l = jax.random.uniform(ks[4], (D_HID, D_OUT), jnp.float32, -s2, s2)
        W2_r = jax.random.uniform(ks[5], (D_HID, D_OUT), jnp.float32, -s2, s2)
        b2 = jnp.zeros((D_OUT,), jnp.float32)
        return {'x': x, 'edge_index': edge_index, 'W1_l': W1_l, 'b1': b1, 'W1_r': W1_r, 'W2_l': W2_l, 'b2': b2, 'W2_r': W2_r}
    _L0_gnn_all = _L0_gnn_setup()
    _L0_gnn_in = {k: v for k, v in _L0_gnn_all.items() if k in ('W1_l', 'b1', 'W1_r', 'W2_l', 'b2', 'W2_r')}
    del _L0_gnn_all

    def _L1_gnn_setup():
        import jax, jax.numpy as jnp
        import numpy as np
        N_NODES = 6250
        N_EDGES = 100000
        D = 96
        key = jax.random.key(seed)
        k_x, k_src, k_dst, k_ws, k_wn = jax.random.split(key, 5)
        x = jax.random.normal(k_x, (N_NODES, D), dtype=jnp.float32)
        src = jax.random.randint(k_src, (N_EDGES,), 0, N_NODES, dtype=jnp.int32)
        dst = jax.random.randint(k_dst, (N_EDGES,), 0, N_NODES, dtype=jnp.int32)
        W_self = jax.random.normal(k_ws, (D, D), dtype=jnp.float32) / np.sqrt(D)
        W_neigh = jax.random.normal(k_wn, (D, D), dtype=jnp.float32) / np.sqrt(D)
        b = jnp.zeros((D,), dtype=jnp.float32)
        return {'x': x, 'src': src, 'dst': dst, 'W_self': W_self, 'W_neigh': W_neigh, 'b': b}
    _L1_gnn_all = _L1_gnn_setup()
    _L1_gnn_in = {k: v for k, v in _L1_gnn_all.items() if k in ('W_self', 'W_neigh', 'b')}
    del _L1_gnn_all

    def _L2_gnn_setup():
        import jax, jax.numpy as jnp
        import numpy as np
        N, E = (6250, 100000)
        DIN = DOUT = 96
        DE = 32

        def _egnn_conv(x, src, dst, edge_attr, W_msg, W_edge, W_root, b):
            msg = x[src] @ W_msg + edge_attr @ W_edge
            agg = jax.ops.segment_max(msg, dst, num_segments=x.shape[0])
            agg = jnp.where(jnp.isneginf(agg), 0.0, agg)
            return agg + x @ W_root + b
        key = jax.random.key(seed)
        ks = jax.random.split(key, 10)
        rn = lambda k, sh, sc: jax.random.normal(k, sh, jnp.float32) * sc
        return {'X': rn(ks[0], (N, DIN), 1.0), 'edge_index': jax.random.randint(ks[1], (2, E), 0, N, jnp.int32), 'edge_attr': rn(ks[2], (E, DE), 1.0), 'W1_msg': rn(ks[3], (DIN, DOUT), DIN ** (-0.5)), 'W1_edge': rn(ks[4], (DE, DOUT), DE ** (-0.5)), 'W1_root': rn(ks[5], (DIN, DOUT), DIN ** (-0.5)), 'b1': jnp.zeros((DOUT,), jnp.float32), 'W2_msg': rn(ks[6], (DOUT, DOUT), DOUT ** (-0.5)), 'W2_edge': rn(ks[7], (DE, DOUT), DE ** (-0.5)), 'W2_root': rn(ks[8], (DOUT, DOUT), DOUT ** (-0.5)), 'b2': jnp.zeros((DOUT,), jnp.float32)}
    _L2_gnn_all = _L2_gnn_setup()
    _L2_gnn_in = {k: v for k, v in _L2_gnn_all.items() if k in ('W1_msg', 'W1_edge', 'W1_root', 'b1', 'W2_msg', 'W2_edge', 'W2_root', 'b2')}
    del _L2_gnn_all

    def _L3_gnn_setup():
        import jax, jax.numpy as jnp
        import numpy as np
        EPS = 1e-05

        def _gcn_conv(x, edge_index, W, b):
            h = x @ W
            src, dst = (edge_index[0], edge_index[1])
            msgs = h[src]
            agg = jax.ops.segment_sum(msgs, dst, num_segments=x.shape[0])
            return agg + b

        def _graph_norm(x, weight, bias, mean_scale):
            mean = jnp.mean(x, axis=0, keepdims=True)
            xc = x - mean_scale * mean
            var = jnp.mean(xc * xc, axis=0, keepdims=True)
            return xc * jax.lax.rsqrt(var + EPS) * weight + bias
        key = jax.random.key(seed)
        ks = jax.random.split(key, 8)
        N, E, D = (6250, 100000, 96)
        x = jax.random.normal(ks[0], (N, D), dtype=jnp.float32)
        edge_index = jax.random.randint(ks[1], (2, E), 0, N, dtype=jnp.int32)
        s = 1.0 / np.sqrt(D)
        W1 = jax.random.normal(ks[2], (D, D), dtype=jnp.float32) * s
        b1 = jnp.zeros((D,), dtype=jnp.float32)
        W2 = jax.random.normal(ks[3], (D, D), dtype=jnp.float32) * s
        b2 = jnp.zeros((D,), dtype=jnp.float32)
        gn1_w = jnp.ones((D,), dtype=jnp.float32)
        gn1_b = jnp.zeros((D,), dtype=jnp.float32)
        gn1_a = jnp.ones((D,), dtype=jnp.float32)
        gn2_w = jnp.ones((D,), dtype=jnp.float32)
        gn2_b = jnp.zeros((D,), dtype=jnp.float32)
        gn2_a = jnp.ones((D,), dtype=jnp.float32)
        return {'x': x, 'edge_index': edge_index, 'W1': W1, 'b1': b1, 'W2': W2, 'b2': b2, 'gn1_w': gn1_w, 'gn1_b': gn1_b, 'gn1_a': gn1_a, 'gn2_w': gn2_w, 'gn2_b': gn2_b, 'gn2_a': gn2_a}
    _L3_gnn_all = _L3_gnn_setup()
    _L3_gnn_in = {k: v for k, v in _L3_gnn_all.items() if k in ('W1', 'b1', 'W2', 'b2', 'gn1_w', 'gn1_b', 'gn1_a', 'gn2_w', 'gn2_b', 'gn2_a')}
    del _L3_gnn_all
    return {'x': x, 'src': src, 'dst': dst, 'edge_attr_32': edge_attr_32, 'L0_gnn_W1_l': _L0_gnn_in['W1_l'], 'L0_gnn_b1': _L0_gnn_in['b1'], 'L0_gnn_W1_r': _L0_gnn_in['W1_r'], 'L0_gnn_W2_l': _L0_gnn_in['W2_l'], 'L0_gnn_b2': _L0_gnn_in['b2'], 'L0_gnn_W2_r': _L0_gnn_in['W2_r'], 'L1_gnn_W_self': _L1_gnn_in['W_self'], 'L1_gnn_W_neigh': _L1_gnn_in['W_neigh'], 'L1_gnn_b': _L1_gnn_in['b'], 'L2_gnn_W1_msg': _L2_gnn_in['W1_msg'], 'L2_gnn_W1_edge': _L2_gnn_in['W1_edge'], 'L2_gnn_W1_root': _L2_gnn_in['W1_root'], 'L2_gnn_b1': _L2_gnn_in['b1'], 'L2_gnn_W2_msg': _L2_gnn_in['W2_msg'], 'L2_gnn_W2_edge': _L2_gnn_in['W2_edge'], 'L2_gnn_W2_root': _L2_gnn_in['W2_root'], 'L2_gnn_b2': _L2_gnn_in['b2'], 'L3_gnn_W1': _L3_gnn_in['W1'], 'L3_gnn_b1': _L3_gnn_in['b1'], 'L3_gnn_W2': _L3_gnn_in['W2'], 'L3_gnn_b2': _L3_gnn_in['b2'], 'L3_gnn_gn1_w': _L3_gnn_in['gn1_w'], 'L3_gnn_gn1_b': _L3_gnn_in['gn1_b'], 'L3_gnn_gn1_a': _L3_gnn_in['gn1_a'], 'L3_gnn_gn2_w': _L3_gnn_in['gn2_w'], 'L3_gnn_gn2_b': _L3_gnn_in['gn2_b'], 'L3_gnn_gn2_a': _L3_gnn_in['gn2_a']}

def reference(x, src, dst, edge_attr_32, L0_gnn_W1_l, L0_gnn_b1, L0_gnn_W1_r, L0_gnn_W2_l, L0_gnn_b2, L0_gnn_W2_r, L1_gnn_W_self, L1_gnn_W_neigh, L1_gnn_b, L2_gnn_W1_msg, L2_gnn_W1_edge, L2_gnn_W1_root, L2_gnn_b1, L2_gnn_W2_msg, L2_gnn_W2_edge, L2_gnn_W2_root, L2_gnn_b2, L3_gnn_W1, L3_gnn_b1, L3_gnn_W2, L3_gnn_b2, L3_gnn_gn1_w, L3_gnn_gn1_b, L3_gnn_gn1_a, L3_gnn_gn2_w, L3_gnn_gn2_b, L3_gnn_gn2_a):
    import jax
    import jax.numpy as jnp

    def _L0_gnn_ref(x, edge_index, W1_l, b1, W1_r, W2_l, b2, W2_r):
        import jax, jax.numpy as jnp
        import numpy as np
        N_NODES = 6250
        N_EDGES = 100000
        D_IN = 96
        D_HID = 96
        D_OUT = 96

        def _sage_layer(h, src, dst, W_l, b_l, W_r):
            msgs = h[src]
            agg = jax.ops.segment_sum(msgs, dst, num_segments=N_NODES)
            cnt = jax.ops.segment_sum(jnp.ones((src.shape[0], 1), h.dtype), dst, num_segments=N_NODES)
            mean = agg / jnp.maximum(cnt, 1.0)
            return mean @ W_l + b_l + h @ W_r
        src, dst = (edge_index[0], edge_index[1])
        h = jax.nn.relu(_sage_layer(x, src, dst, W1_l, b1, W1_r))
        out = _sage_layer(h, src, dst, W2_l, b2, W2_r)
        return out

    def _L1_gnn_ref(x, src, dst, W_self, W_neigh, b):
        import jax, jax.numpy as jnp
        import numpy as np
        N_NODES = 6250
        N_EDGES = 100000
        D = 96
        n = x.shape[0]
        msg = x[src]
        neigh_sum = jax.ops.segment_sum(msg, dst, num_segments=n)
        deg = jax.ops.segment_sum(jnp.ones(src.shape, x.dtype), dst, num_segments=n)
        h_neigh = neigh_sum / jnp.maximum(deg, 1.0)[:, None]
        return x @ W_self + h_neigh @ W_neigh + b

    def _L2_gnn_ref(X, edge_index, edge_attr, W1_msg, W1_edge, W1_root, b1, W2_msg, W2_edge, W2_root, b2):
        import jax, jax.numpy as jnp
        import numpy as np
        N, E = (6250, 100000)
        DIN = DOUT = 96
        DE = 32

        def _egnn_conv(x, src, dst, edge_attr, W_msg, W_edge, W_root, b):
            msg = x[src] @ W_msg + edge_attr @ W_edge
            agg = jax.ops.segment_max(msg, dst, num_segments=x.shape[0])
            agg = jnp.where(jnp.isneginf(agg), 0.0, agg)
            return agg + x @ W_root + b
        src, dst = (edge_index[0], edge_index[1])
        c1 = jax.nn.leaky_relu(_egnn_conv(X, src, dst, edge_attr, W1_msg, W1_edge, W1_root, b1))
        c2 = jax.nn.leaky_relu(_egnn_conv(c1, src, dst, edge_attr, W2_msg, W2_edge, W2_root, b2))
        return c2

    def _L3_gnn_ref(x, edge_index, W1, b1, W2, b2, gn1_w, gn1_b, gn1_a, gn2_w, gn2_b, gn2_a):
        import jax, jax.numpy as jnp
        import numpy as np
        EPS = 1e-05

        def _gcn_conv(x, edge_index, W, b):
            h = x @ W
            src, dst = (edge_index[0], edge_index[1])
            msgs = h[src]
            agg = jax.ops.segment_sum(msgs, dst, num_segments=x.shape[0])
            return agg + b

        def _graph_norm(x, weight, bias, mean_scale):
            mean = jnp.mean(x, axis=0, keepdims=True)
            xc = x - mean_scale * mean
            var = jnp.mean(xc * xc, axis=0, keepdims=True)
            return xc * jax.lax.rsqrt(var + EPS) * weight + bias
        identity = x
        h = _gcn_conv(x, edge_index, W1, b1)
        h = _graph_norm(h, gn1_w, gn1_b, gn1_a)
        h = jax.nn.relu(h)
        h = h + identity
        identity = h
        h2 = _gcn_conv(h, edge_index, W2, b2)
        h2 = _graph_norm(h2, gn2_w, gn2_b, gn2_a)
        h2 = jax.nn.relu(h2)
        h2 = h2 + identity
        return h2
    edge_index = jnp.stack([src, dst])
    h = jnp.maximum(_layernorm(x, axis=-1), 0.0)
    x = x + _L0_gnn_ref(h, edge_index, L0_gnn_W1_l, L0_gnn_b1, L0_gnn_W1_r, L0_gnn_W2_l, L0_gnn_b2, L0_gnn_W2_r)
    h = jnp.maximum(_layernorm(x, axis=-1), 0.0)
    x = x + _L1_gnn_ref(h, src, dst, L1_gnn_W_self, L1_gnn_W_neigh, L1_gnn_b)
    h = jnp.maximum(_layernorm(x, axis=-1), 0.0)
    x = x + _L2_gnn_ref(h, edge_index, edge_attr_32, L2_gnn_W1_msg, L2_gnn_W1_edge, L2_gnn_W1_root, L2_gnn_b1, L2_gnn_W2_msg, L2_gnn_W2_edge, L2_gnn_W2_root, L2_gnn_b2)
    h = jnp.maximum(_layernorm(x, axis=-1), 0.0)
    x = x + _L3_gnn_ref(h, edge_index, L3_gnn_W1, L3_gnn_b1, L3_gnn_W2, L3_gnn_b2, L3_gnn_gn1_w, L3_gnn_gn1_b, L3_gnn_gn1_a, L3_gnn_gn2_w, L3_gnn_gn2_b, L3_gnn_gn2_a)
    return x

_drawn_inputs = setup_inputs


def setup_inputs(seed=0):
    import zlib

    import numpy as np

    out = dict(_drawn_inputs(seed))
    spreads = {'L0_gnn_b1': (0.0, 0.449),
     'L0_gnn_b2': (0.0, 0.1),
     'L1_gnn_b': (0.0, 0.1),
     'L2_gnn_b1': (0.0, 0.301),
     'L2_gnn_b2': (0.0, 0.431),
     'L3_gnn_b1': (0.0, 0.8),
     'L3_gnn_b2': (0.0, 0.8),
     'L3_gnn_gn1_w': (1.0, 0.2),
     'L3_gnn_gn1_b': (0.0, 0.522),
     'L3_gnn_gn1_a': (1.0, 0.2),
     'L3_gnn_gn2_w': (1.0, 0.6),
     'L3_gnn_gn2_b': (0.0, 0.609),
     'L3_gnn_gn2_a': (1.0, 0.2)}
    factors = {}
    for name, (base, spread) in spreads.items():
        noise = np.random.default_rng([zlib.crc32(name.encode()), seed]).standard_normal(out[name].shape)
        drawn = base * np.exp(spread * noise) if base else spread * noise
        out[name] = jnp.asarray(drawn.astype(out[name].dtype))
    for name, factor in factors.items():
        out[name] = (out[name] * factor).astype(out[name].dtype)
    return out
```

```python
from contextlib import ExitStack

import concourse.bass as bass
from concourse import mybir

P = 128
N, E, D, DE = 6250, 200000, 96, 32
TILES = -(-N // P)
NPAD = TILES * P
GROUP = 7
GROUPS = TILES // GROUP
HALF = 16
STEP = 2 * HALF
STEPS = -(-E // (P * STEP))
SLOTS = STEPS * STEP
TAIL = E - (P - 1) * SLOTS
MAIN, REST = 112, 15
QUAD = P // DE
BIG = 3.4028235e38
PAD_NODE = NPAD - 1
EPS = 1e-5

WEIGHTS = ["L0_gnn_W1_l", "L0_gnn_W1_r", "L0_gnn_W2_l", "L0_gnn_W2_r", "L1_gnn_W_self",
           "L1_gnn_W_neigh", "L2_gnn_W1_msg", "L2_gnn_W1_root", "L2_gnn_W2_msg",
           "L2_gnn_W2_root", "L3_gnn_W1", "L3_gnn_W2"]
BIASES = {"L0_gnn_W1_l": "L0_gnn_b1", "L0_gnn_W2_l": "L0_gnn_b2", "L1_gnn_W_self": "L1_gnn_b",
          "L2_gnn_W1_root": "L2_gnn_b1", "L2_gnn_W2_root": "L2_gnn_b2",
          "L3_gnn_W1": "L3_gnn_b1", "L3_gnn_W2": "L3_gnn_b2"}
NORMS = ["L3_gnn_gn1_w", "L3_gnn_gn1_b", "L3_gnn_gn1_a", "L3_gnn_gn2_w", "L3_gnn_gn2_b",
         "L3_gnn_gn2_a"]

STAGES = [
    ("setup",),
    ("norm",),
    ("edges", "h", "sum", "mean"),
    ("project", [("agg", "L0_gnn_W1_l"), ("h", "L0_gnn_W1_r")], "relu", "h2"),
    ("edges", "h2", "sum", "mean"),
    ("project", [("agg", "L0_gnn_W2_l"), ("h2", "L0_gnn_W2_r")], "add", "x"),
    ("norm",),
    ("edges", "h", "sum", "mean"),
    ("project", [("h", "L1_gnn_W_self"), ("agg", "L1_gnn_W_neigh")], "add", "x"),
    ("norm",),
    ("project", [("h", "L2_gnn_W1_msg")], "copy", "agg"),
    ("edges", "agg", "max", "some"),
    ("project", [("h", "L2_gnn_W1_root")], "leaky", "h2"),
    ("project", [("h2", "L2_gnn_W2_msg")], "copy", "agg"),
    ("edges", "agg", "max", "some"),
    ("project", [("h2", "L2_gnn_W2_root")], "leaky_add", "x"),
    ("norm",),
    ("edges", "h", "sum", "some"),
    ("project", [("agg", "L3_gnn_W1")], "copy", "agg2"),
    ("graphnorm", 0, "h", "h2"),
    ("edges", "h2", "sum", "some"),
    ("project", [("agg", "L3_gnn_W2")], "copy", "agg2"),
    ("graphnorm", 1, "h2", "x"),
]


def numbered():
    seen = {}
    for i, s in enumerate(STAGES):
        yield i, seen.get(s[0], 0), s
        seen[s[0]] = seen.get(s[0], 0) + 1


PASSES = [s for s in STAGES if s[0] == "edges"]
MAX_PASS = [sum(s[2] == "max" for s in PASSES[:k]) for k in range(len(PASSES))]


class Chain:

    def __init__(self, engine, sem):
        self.engine, self.sem, self.n, self.reg, self.per = engine, sem, 0, None, 0

    def __call__(self, ins):
        self.n += 1
        ins.then_inc(self.sem, 1)
        self.engine.wait_ge(self.sem, self.n if self.reg is None else self.reg * self.per + self.n)

    def enter(self, reg, per):
        self.reg, self.per, self.at = reg, per, self.n

    def leave(self, trips):
        assert self.n == self.at + self.per
        self.n, self.reg = self.at + self.per * trips, None


def build(nc, a, out):
    f32, bf16, i32 = mybir.dt.float32, mybir.dt.bfloat16, mybir.dt.int32
    ALU = mybir.AluOpType
    ACT = mybir.ActivationFunctionType
    AX = mybir.AxisListType

    with ExitStack() as ctx:
        def sb(name, shape, dt=f32):
            return ctx.enter_context(nc.sbuf_tensor(name, shape, dt))

        def sem(name):
            return ctx.enter_context(nc.semaphore(name))

        table = nc.dram_tensor("table", (NPAD, D), f32, kind="Internal").ap()
        running = nc.dram_tensor("running", (P * SLOTS, D), f32, kind="Internal").ap()
        edge_tail = nc.dram_tensor("edge_tail", (SLOTS, DE), f32, kind="Internal").ap()

        x = sb("x_sb", [P, TILES, D])
        h = sb("h_sb", [P, TILES, D])
        h2 = sb("h2_sb", [P, TILES, D])
        agg = sb("agg_sb", [P, TILES, D])
        tmp = sb("tmp_sb", [P, TILES, D])
        node_tile = {"x": x, "h": h, "h2": h2, "agg": agg, "agg2": tmp}
        src = sb("src_sb", [P, SLOTS + STEP], i32)
        dst_f = sb("dst_f", [P, SLOTS])
        keep = sb("keep", [P, SLOTS])
        dst_lo = sb("dst_lo", [P, SLOTS], bf16)
        dst_hi = sb("dst_hi", [P, SLOTS], bf16)
        idx_stage = sb("idx_stage", [P, 2, HALF], i32)
        keep_stage = sb("keep_stage", [P, 2, HALF])
        msg = sb("msg", [P, 2, HALF, D])
        run = sb("run", [P, 2, HALF, D])
        ea = sb("ea", [P, 2, HALF, DE])
        eaT = sb("eaT", [P, 2, HALF // QUAD, P])
        fix_row = sb("fix_row", [P, D])
        fixed = sb("fixed", [P, D])
        chainT = sb("chainT", [D, P + 1])
        ident = sb("ident", [P, P])
        ones = sb("ones", [P, P])
        upto = sb("upto", [P, P])
        iota_i = sb("iota_i", [P, P], i32)
        iota_b = sb("iota_b", [P, P], bf16)
        zeros_b = sb("zeros_b", [P, P], bf16)
        lo_hot = sb("lo_hot", [P, 2, HALF, P], bf16)
        hi_hot = sb("hi_hot", [P, 2, HALF, TILES], bf16)
        count = sb("count", [P, TILES])
        total = sb("total", [P, TILES])
        before = sb("before", [P, TILES])
        end_f = sb("end_f", [P, TILES])
        end_i = sb("end_i", [P, TILES], i32)
        some = sb("some", [P, TILES])
        mean_scale = sb("mean_scale", [P, TILES])
        stat = sb("stat", [P, 2, TILES])
        prev_i = sb("prev_i", [P, 1], i32)
        col = sb("col", [P, 8])
        first_i = sb("first_i", [P, 1], i32)
        start_i = sb("start_i", [P, 1], i32)
        wide = sb("wide", [P, D])
        crossT = sb("crossT", [D, P])
        w_all = sb("w_all", [D + 1, len(WEIGHTS), D])
        w_edge = sb("w_edge", [P, 2, QUAD, D])
        norm_p = sb("norm_p", [P, len(NORMS), D])
        node_stage = sb("node_stage", [P, 2, GROUP, D])
        nodeT = sb("nodeT", [D + 1, 2, GROUP, P])
        g_sum = sb("g_sum", [P, D])
        g_a = sb("g_a", [P, D])
        g_b = sb("g_b", [P, D])
        g_c = sb("g_c", [P, D])
        ps = ctx.enter_context(nc.psum_tensor("ps", [P, 8, 512], f32))

        ps_nodeT = [ps[0:D, 2 * i:2 * i + 2, :].rearrange("p b (t n) -> p (b t) n", n=P)[:, 0:GROUP, :]
                    for i in range(2)]
        ps_out = ps[:, 4:6, :].rearrange("p b (t n) -> p (b t) n", n=P)[:, 0:GROUP, 0:D]
        ps_outw = ps[:, 4:6, :].rearrange("p b (t n) -> p (b t) n", n=P)
        ps_eaT = [ps[:, i, :].rearrange("p (q n) -> p q n", n=P) for i in range(2)]
        ps_edge = ps[:, 2:6, 0:QUAD * D]
        ps_count = ps[:, 6, 0:TILES]
        ps_cum = ps[:, 6, 64:64 + TILES]
        ps_tot = ps[:, 6, 128:128 + TILES]
        ps_lastT = ps[0:D, 7, 0:P]
        ps_carry = ps[:, 7, 128:128 + D]
        ps_stat = ps[:, 7, 256:256 + D]

        stage_done = sem("stage_done")
        dve_done = sem("dve_done")
        loaded = sem("loaded")
        dst_loaded = sem("dst_loaded")
        zeroed = sem("zeroed")
        ready = sem("constants_ready")
        pool_made = sem("pool_made")
        hot_ready = sem("hot_ready")
        hot_used = sem("hot_used")
        count_ready = sem("count_ready")
        count_copied = sem("count_copied")
        cum_ready = sem("cum_ready")
        wide_ready = sem("wide_ready")
        wideT_ready = sem("wideT_ready")
        staged = sem("staged")
        transposed = sem("transposed")
        lhs_ready = sem("lhs_ready")
        projected = sem("projected")
        drained = sem("drained")
        std_in = sem("std_in")
        std_out = sem("std_out")
        sum_in = sem("sum_in")
        sum_out = sem("sum_out")
        table_stored = sem("table_stored")
        idx_ready = [sem(f"idx_ready{i}") for i in range(2)]
        gathered = [[sem(f"gathered{k}_{i}") for i in range(2)] for k in range(len(PASSES))]
        scanned = [sem(f"scanned{i}") for i in range(2)]
        stored = [sem(f"stored{i}") for i in range(2)]
        ea_loaded = [sem(f"ea_loaded{i}") for i in range(2)]
        ea_turned = [sem(f"ea_turned{i}") for i in range(2)]
        eaT_ready = [sem(f"eaT_ready{i}") for i in range(2)]
        edge_ready = [sem(f"edge_ready{i}") for i in range(2)]
        edge_used = sem("edge_used")
        lastT_ready = sem("lastT_ready")
        chain_ready = sem("chain_ready")
        carry_ready = sem("carry_ready")
        row_gathered = sem("row_gathered")
        row_fixed = sem("row_fixed")
        row_stored = sem("row_stored")
        agg_gathered = sem("agg_gathered")
        out_stored = sem("out_stored")
        half_open = sem("half_open")

        EDGE_PARTS = [(0, MAIN), (MAIN, P - 1), (P - 1, P)]

        def by_tile(v):
            return v.rearrange("(t p) f -> p t f", p=P)

        running_rows = running.rearrange("(p s) f -> p (s f)", p=P)
        dst_i = tmp[:, :, :].bitcast(i32).rearrange("p t f -> p (t f)")[:, 0:SLOTS]
        part_i = agg[:, :, :].bitcast(i32).rearrange("p t f -> p (t f)")[:, 0:SLOTS]
        scratch = h[:, :, :].rearrange("p t f -> p (t f)")[:, 0:SLOTS]
        valid, prev_f, join, full, cross, first_n, first_f, start_f = (col[:, i:i + 1] for i in range(8))
        LAST = TILES - 1
        LAST_N = N - LAST * P

        block = ctx.enter_context(nc.Block())

        @block.sync
        def _(sp):
            def load_edges(to, v, done):
                for p0, p1 in EDGE_PARTS:
                    part = v[p0 * SLOTS:min(p1 * SLOTS, E)]
                    w = part.shape[0] // (p1 - p0)
                    sp.dma_start(to[p0:p1, 0:w], part.rearrange("(p s) -> p s", s=w)).then_inc(done, 16)

            def store_running(r, hf, k):
                sp.wait_ge(scanned[hf], r + STEPS * k + 2)
                sp.dma_start(running_rows[:, bass.ds(r * (STEP * D) + hf * HALF * D, HALF * D)],
                             run[:, hf, :, :].rearrange("p s f -> p (s f)")).then_inc(stored[hf], 16)

            def load_attributes(r, hf):
                at = bass.ds(r * (STEP * DE) + hf * HALF * DE, HALF * DE)
                for p0, p1 in EDGE_PARTS:
                    v = a["edge_attr_32"][p0 * SLOTS:p1 * SLOTS, :] if p1 < P else edge_tail
                    sp.dma_start(ea[p0:p1, hf, :, :].rearrange("p s f -> p (s f)"),
                                 v.rearrange("(p s) f -> p (s f)", s=SLOTS)[:, at]).then_inc(ea_loaded[hf], 16)

            sp.wait_ge(zeroed, 1)
            for hf in range(2):
                sp.dma_start(running_rows[:, hf * HALF * D:(hf + 1) * HALF * D],
                             run[:, hf, :, :].rearrange("p s f -> p (s f)")).then_inc(stored[hf], 16)
            load_edges(dst_i, a["dst"], dst_loaded)
            with nc.allow_non_contiguous_dma(reason="one word for each partition"):
                sp.dma_start(prev_i[1:P, :], a["dst"][SLOTS - 1:(P - 1) * SLOTS:SLOTS].unsqueeze(1)
                             ).then_inc(dst_loaded, 16)
            load_edges(src, a["src"], loaded)
            sp.dma_start(x[:, 0:LAST, :], by_tile(a["x"][0:LAST * P, :])).then_inc(loaded, 16)
            sp.dma_start(x[0:LAST_N, LAST, :], a["x"][LAST * P:N, :]).then_inc(loaded, 16)
            sp.dma_start(edge_tail[0:TAIL, :], a["edge_attr_32"][E - TAIL:E, :]).then_inc(loaded, 16)
            sp.dma_start(edge_tail[TAIL:SLOTS, :].rearrange("(p q) f -> p (q f)", p=64),
                         run[0:64, :, :, :].rearrange("p a s f -> p (a s f)")[:, 0:(SLOTS - TAIL) * DE // 64]
                         ).then_inc(loaded, 16)
            for i, name in enumerate(WEIGHTS):
                sp.dma_start(w_all[0:D, i, :], a[name]).then_inc(loaded, 16)
                if name in BIASES:
                    sp.dma_start(w_all[D:D + 1, i, :], a[BIASES[name]].unsqueeze(0)).then_inc(loaded, 16)
            for i, name in enumerate(("L2_gnn_W1_edge", "L2_gnn_W2_edge")):
                for q in range(QUAD):
                    sp.dma_start(w_edge[q * DE:(q + 1) * DE, i, q, :], a[name]).then_inc(loaded, 16)
            for i, name in enumerate(NORMS):
                sp.dma_start(norm_p[:, i, :], a[name].unsqueeze(0).to_broadcast([P, D])).then_inc(loaded, 16)

            for i, k, stage in numbered():
                if stage[0] != "edges":
                    continue
                sp.wait_ge(stage_done, i)
                sp.dma_start(by_tile(table), node_tile[stage[1]][:, :, :]).then_inc(table_stored, 16)
                if stage[2] == "sum":
                    with sp.Fori(0, STEPS) as r:
                        for hf in range(2):
                            store_running(r, hf, k)
                else:
                    m = MAX_PASS[k]
                    for hf in range(2):
                        load_attributes(0, hf)
                    with sp.Fori(0, STEPS - 1) as r:
                        for hf in range(2):
                            store_running(r, hf, k)
                            sp.wait_ge(ea_turned[hf], r + STEPS * m + 1)
                            load_attributes(r + 1, hf)
                    for hf in range(2):
                        store_running(STEPS - 1, hf, k)
            sp.wait_ge(stage_done, len(STAGES))
            sp.dma_start(by_tile(out[0:LAST * P, :]), x[:, 0:LAST, :]).then_inc(out_stored, 16)
            sp.dma_start(out[LAST * P:N, :], x[0:LAST_N, LAST, :]).then_inc(out_stored, 16)
            sp.wait_ge(out_stored, 32)

        @block.gpsimd
        def _(pool):
            pool.memset(ident[:, :], 0.0)
            pool.memset(upto[:, :], 1.0).then_inc(pool_made, 1)
            pool.wait_ge(pool_made, 1)
            pool.affine_select(out=ident[:, :], in_=ident[:, :], compare_op=ALU.not_equal, fill=1.0,
                               base=0, pattern=[[-1, P]], channel_multiplier=1)
            pool.affine_select(out=upto[:, :], in_=upto[:, :], compare_op=ALU.is_ge, fill=0.0,
                               base=0, pattern=[[1, P]], channel_multiplier=-1)
            pool.iota(iota_i[:, :], pattern=[[1, P]], base=0, channel_multiplier=0)
            pool.iota(start_i[:, :], pattern=[[0, 1]], base=0, channel_multiplier=SLOTS).then_inc(ready, 1)

            def gather(to, frm, idx, done):
                pool.indirect_dma_start(to, None, frm, bass.IndirectOffsetOnAxis(ap=idx, axis=0)
                                        ).then_inc(done, 16)

            for i, k, stage in numbered():
                if stage[0] != "edges":
                    continue
                with pool.Fori(0, STEPS) as r:
                    for hf in range(2):
                        pool.wait_ge(table_stored, 16 * (k + 1))
                        pool.wait_ge(idx_ready[hf], r + (STEPS + 1) * k + 1)
                        pool.wait_ge(scanned[hf], r + STEPS * k + 1)
                        pool.sem_inc(half_open, 1)
                        for s in range(HALF):
                            gather(msg[:, hf, s, :], table, idx_stage[:, hf, s:s + 1], gathered[k][hf])
                for hf in range(2):
                    pool.wait_ge(stored[hf], 16 * STEPS * (k + 1) + 16)
                gather(fix_row[:, :], running, first_i[:, :], row_gathered)
                pool.wait_ge(row_fixed, k + 1)
                pool.indirect_dma_start(running, bass.IndirectOffsetOnAxis(ap=first_i[:, :], axis=0),
                                        fixed[:, :], None).then_inc(row_stored, 16)
                pool.wait_ge(row_stored, 16 * (k + 1))
                for t in range(TILES):
                    gather(agg[:, t, :], running, end_i[:, t:t + 1], agg_gathered)

        @block.scalar
        def _(act):
            for s in (lhs_ready, *eaT_ready):
                act.sem_inc(s, 1)
            roots = 0
            for i, k, stage in numbered():
                act.wait_ge(stage_done, i)
                if stage[0] in ("norm", "graphnorm"):
                    roots += 1
                    v = stat[:, 1, :] if stage[0] == "norm" else g_b[:, :]
                    act.wait_ge(std_in, roots)
                    act.activation(v, v, ACT.Sqrt).then_inc(std_out, 1)
                elif stage[0] == "project":
                    n = len(stage[1])
                    with act.Fori(0, GROUPS) as r:
                        act.wait_ge(transposed, r + GROUPS * k + 1)
                        for j, (name, _) in enumerate(stage[1]):
                            last = act.copy(node_stage[:, j, :, :],
                                            node_tile[name][:, bass.ds(r * GROUP, GROUP), :])
                        last.then_inc(staged, 1)
                        act.wait_ge(transposed, r + GROUPS * k + 2)
                        act.wait_ge(projected, r + GROUPS * k + 1)
                        for j in range(n):
                            last = act.copy(nodeT[0:D, j, :, :], ps_nodeT[j])
                        last.then_inc(lhs_ready, 1)
                elif stage[0] == "edges" and stage[2] == "max":
                    m = MAX_PASS[k]
                    with act.Fori(0, STEPS) as r:
                        for hf in range(2):
                            act.wait_ge(ea_turned[hf], r + STEPS * m + 1)
                            act.wait_ge(edge_ready[hf], r + STEPS * m + 1)
                            act.copy(eaT[:, hf, :, :], ps_eaT[hf]).then_inc(eaT_ready[hf], 1)

        @block.tensor
        def _(pe):
            for s in (transposed, projected, hot_used, *edge_ready):
                pe.sem_inc(s, 1)
            pe.wait_ge(ready, 1)
            pe.wait_ge(zeroed, 1)
            pe.matmul(ps_count, zeros_b[:, :], zeros_b[:, 0:TILES], start=True, stop=False)
            with pe.Fori(0, STEPS) as r:
                for hf in range(2):
                    pe.wait_ge(hot_ready, r * 2 + hf + 1)
                    for s in range(HALF):
                        last = pe.matmul(ps_count, lo_hot[:, hf, s, :], hi_hot[:, hf, s, :],
                                         start=False, stop=False)
                    last.then_inc(hot_used, 1)
            pe.matmul(ps_count, zeros_b[:, :], zeros_b[:, 0:TILES], start=False, stop=True).then_inc(count_ready, 1)
            pe.wait_ge(count_copied, 1)
            pe.matmul(ps_cum, upto[:, :], count[:, :], start=True, stop=True)
            pe.matmul(ps_tot, ones[:, :], count[:, :], start=True, stop=True).then_inc(cum_ready, 1)
            pe.wait_ge(wide_ready, 1)
            pe.transpose(ps_lastT, wide[:, :], ident[:, :]).then_inc(wideT_ready, 1)
            sums = 0
            for i, k, stage in numbered():
                pe.wait_ge(stage_done, i)
                if stage[0] == "graphnorm":
                    for _ in range(2):
                        sums += 1
                        pe.wait_ge(sum_in, sums)
                        pe.matmul(ps_stat, ones[:, :], g_sum[:, :], start=True, stop=True).then_inc(sum_out, 1)
                elif stage[0] == "project":
                    n = len(stage[1])
                    with pe.Fori(0, GROUPS) as r:
                        pe.wait_ge(staged, r + GROUPS * k + 1)
                        pe.wait_ge(lhs_ready, r + GROUPS * k + 1)
                        for j in range(n):
                            for t in range(GROUP):
                                last = pe.transpose(ps_nodeT[j][:, t, :], node_stage[:, j, t, :], ident[:, :])
                        last.then_inc(transposed, 1)
                        pe.wait_ge(lhs_ready, r + GROUPS * k + 2)
                        pe.wait_ge(drained, r + GROUPS * k + 1)
                        for t in range(GROUP):
                            for j, (_, w) in enumerate(stage[1]):
                                last = pe.matmul(ps_out[:, t, :], nodeT[:, j, t, :], w_all[:, WEIGHTS.index(w), :],
                                                 start=(j == 0), stop=(j == n - 1))
                        last.then_inc(projected, 1)
                elif stage[0] == "edges":
                    if stage[2] == "max":
                        m = MAX_PASS[k]
                        with pe.Fori(0, STEPS) as r:
                            for hf in range(2):
                                pe.wait_ge(ea_loaded[hf], r * 48 + 48 * (STEPS * m + 1))
                                pe.wait_ge(eaT_ready[hf], r + STEPS * m + 1)
                                for g in range(HALF // QUAD):
                                    last = pe.transpose(ps_eaT[hf][:, g, :],
                                                        ea[:, hf, g * QUAD:(g + 1) * QUAD, :].rearrange("p s f -> p (s f)"),
                                                        ident[:, :])
                                last.then_inc(ea_turned[hf], 1)
                                pe.wait_ge(eaT_ready[hf], r + STEPS * m + 2)
                                pe.wait_ge(edge_used, r * 2 + 2 * STEPS * m + hf + 1)
                                for g in range(HALF // QUAD):
                                    last = pe.matmul(ps_edge[:, g, :], eaT[:, hf, g, :],
                                                     w_edge[:, m, :, :].rearrange("p q f -> p (q f)"),
                                                     start=True, stop=True)
                                last.then_inc(edge_ready[hf], 1)
                    pe.wait_ge(scanned[1], STEPS * (k + 1) + 1)
                    pe.transpose(ps_lastT, run[:, 1, HALF - 1, :], ident[:, :]).then_inc(lastT_ready, 1)
                    pe.wait_ge(chain_ready, k + 1)
                    pe.transpose(ps_carry, chainT[:, 0:P], ident[0:D, 0:D]).then_inc(carry_ready, 1)

        @block.vector
        def _(dve):
            chain = Chain(dve, dve_done)
            for s in (drained, edge_used, *scanned):
                dve.sem_inc(s, 1)

            def end_stage(ins, i):
                ins.then_inc(stage_done, 1)
                dve.wait_ge(stage_done, i + 1)

            def over_tiles(v):
                return v.unsqueeze(1).to_broadcast([P, TILES, D])

            def over_features(v):
                return v.unsqueeze(2).to_broadcast([P, TILES, D])

            for v, value in ((src, 0), (dst_i, PAD_NODE), (prev_i, -1), (zeros_b, 0.0), (ones, 1.0),
                             (w_edge, 0.0), (w_all[D:D + 1, :, :], 0.0), (nodeT[D:D + 1, :, :, :], 1.0),
                             (chainT[:, 0:1], 0.0), (run, 0.0), (x[:, LAST, :], 0.0), (keep[:, 0:1], 0.0)):
                last = dve.memset(v if isinstance(v, bass.AP) else v[tuple(slice(None) for _ in v.shape)], value)
            last.then_inc(zeroed, 1)
            dve.wait_ge(zeroed, 1)
            dve.wait_ge(ready, 1)
            chain(dve.tensor_copy(iota_b[:, :], iota_i[:, :]))
            dve.wait_ge(dst_loaded, 64)
            chain(dve.tensor_copy(dst_f[:, :], dst_i))
            chain(dve.tensor_scalar(part_i, dst_i, 7, None, ALU.arith_shift_right))
            chain(dve.tensor_copy(dst_hi[:, :], part_i))
            chain(dve.tensor_scalar(part_i, dst_i, P - 1, None, ALU.bitwise_and))
            chain(dve.tensor_copy(dst_lo[:, :], part_i))
            chain(dve.tensor_tensor(keep[:, 1:SLOTS], dst_f[:, 1:SLOTS], dst_f[:, 0:SLOTS - 1], ALU.is_equal))
            chain(dve.tensor_copy(start_f, start_i[:, :]))
            chain(dve.tensor_scalar(valid, start_f, float(LAST_N * SLOTS), None, ALU.is_lt))
            chain(dve.tensor_copy(prev_f, prev_i[:, :]))
            chain(dve.tensor_tensor(join, dst_f[:, 0:1], prev_f, ALU.is_equal))
            chain(dve.tensor_tensor(full, dst_f[:, 0:1], dst_f[:, SLOTS - 1:SLOTS], ALU.is_equal))
            chain(dve.tensor_tensor(cross, join, full, ALU.mult))
            chain(dve.tensor_scalar(scratch, dst_f[:, :], dst_f[:, 0:1], None, ALU.is_equal, ALU.add,
                                    accum_out=first_n))
            chain(dve.tensor_tensor(first_f, start_f, first_n, ALU.add))
            chain(dve.tensor_scalar(first_f, first_f, -1.0, None, ALU.add))
            chain(dve.tensor_copy(first_i[:, :], first_f))
            dve.tensor_copy(wide[:, :], cross.to_broadcast([P, D])).then_inc(wide_ready, 1)
            with dve.Fori(0, STEPS) as r:
                for hf in range(2):
                    at = bass.ds(r * STEP + hf * HALF, HALF)
                    if hf == 0:
                        dve.wait_ge(hot_used, r * 2 + 1)
                    dve.tensor_tensor(lo_hot[:, hf, :, :], iota_b[:, :].unsqueeze(1).to_broadcast([P, HALF, P]),
                                      dst_lo[:, at].unsqueeze(2).to_broadcast([P, HALF, P]), ALU.is_equal)
                    dve.tensor_tensor(hi_hot[:, hf, :, :],
                                      iota_b[:, 0:TILES].unsqueeze(1).to_broadcast([P, HALF, TILES]),
                                      dst_hi[:, at].unsqueeze(2).to_broadcast([P, HALF, TILES]), ALU.is_equal
                                      ).then_inc(hot_ready, 1)
            dve.wait_ge(count_ready, 1)
            dve.tensor_copy(count[:, :], ps_count).then_inc(count_copied, 1)
            dve.wait_ge(count_copied, 1)
            dve.wait_ge(cum_ready, 1)
            chain(dve.tensor_copy(total[:, :], ps_tot))
            chain(dve.tensor_tensor_scan(before[:, :], ones[:, 0:TILES], total[:, :], 0.0, ALU.mult, ALU.add))
            chain(dve.tensor_tensor(before[:, :], before[:, :], total[:, :], ALU.subtract))
            chain(dve.tensor_tensor(end_f[:, :], before[:, :], ps_cum, ALU.add))
            chain(dve.tensor_scalar(end_f[:, :], end_f[:, :], -1.0, 0.0, ALU.add, ALU.max))
            chain(dve.tensor_copy(end_i[:, :], end_f[:, :]))
            chain(dve.tensor_scalar(some[:, :], count[:, :], 0.0, None, ALU.is_gt))
            chain(dve.tensor_scalar(mean_scale[:, :], count[:, :], 1.0, None, ALU.max))
            chain(dve.reciprocal(mean_scale[:, :], mean_scale[:, :]))
            chain(dve.tensor_tensor(mean_scale[:, :], mean_scale[:, :], some[:, :], ALU.mult))
            dve.wait_ge(wideT_ready, 1)
            chain(dve.tensor_copy(crossT[:, :], ps_lastT))
            dve.wait_ge(loaded, 16 * (3 + 4 + len(WEIGHTS) + len(BIASES) + 2 * QUAD + len(NORMS)))
            end_stage(dve.tensor_copy(idx_stage[:, 0, 0:1], src[:, 0:1]), 0)

            masks = [keep[:, :], crossT[:, :], join]
            roots = sums = groups = 0
            for i, k, stage in numbered():
                if stage[0] == "norm":
                    roots += 1
                    m, v = stat[:, 0, :], stat[:, 1, :]
                    chain(dve.tensor_reduce(m, x[:, :, :], AX.X, ALU.add))
                    chain(dve.tensor_scalar(m, m, -1.0 / D, None, ALU.mult))
                    chain(dve.tensor_tensor(tmp[:, :, :], x[:, :, :], over_features(m), ALU.add))
                    chain(dve.tensor_tensor(h[:, :, :], tmp[:, :, :], tmp[:, :, :], ALU.mult))
                    chain(dve.tensor_reduce(v, h[:, :, :], AX.X, ALU.add))
                    dve.tensor_scalar(v, v, 1.0 / D, EPS, ALU.mult, ALU.add).then_inc(std_in, 1)
                    dve.wait_ge(std_out, roots)
                    chain(dve.reciprocal(v, v))
                    chain(dve.tensor_tensor(h[:, :, :], tmp[:, :, :], over_features(v), ALU.mult))
                    end_stage(dve.tensor_scalar(h[:, :, :], h[:, :, :], 0.0, None, ALU.max), i)

                elif stage[0] == "project":
                    _, _, how, to = stage
                    to = node_tile[to]
                    steps = {"relu": 0, "add": 0, "copy": 0, "leaky": 1, "leaky_add": 2}[how]
                    with dve.Fori(0, GROUPS) as r:
                        chain.enter(r, steps)
                        at = (slice(None), bass.ds(r * GROUP, GROUP), slice(None))
                        dve.wait_ge(projected, r + GROUPS * k + 2)
                        if how == "relu":
                            last = dve.tensor_scalar(to[at], ps_out, 0.0, None, ALU.max)
                        elif how == "add":
                            last = dve.tensor_tensor(to[at], to[at], ps_out, ALU.add)
                        elif how == "copy":
                            last = dve.tensor_copy(to[at], ps_out)
                        else:
                            chain(dve.tensor_tensor(tmp[at], agg[at], ps_out, ALU.add))
                            c = h2 if how == "leaky" else tmp
                            last = dve.scalar_tensor_tensor(out=c[at], in0=tmp[at], scalar=0.01, in1=tmp[at],
                                                            op0=ALU.mult, op1=ALU.max)
                            if how == "leaky_add":
                                chain(last)
                                last = dve.tensor_tensor(x[at], x[at], tmp[at], ALU.add)
                        last.then_inc(drained, 1)
                        chain.leave(GROUPS)
                    dve.wait_ge(drained, GROUPS * (k + 1) + 1)
                    end_stage(dve.tensor_copy(col[:, 7:8], col[:, 7:8]), i)

                elif stage[0] == "graphnorm":
                    _, which, identity, to = stage
                    w, b, scale = (norm_p[:, 3 * which + j, :] for j in range(3))

                    def mask_pads():
                        chain(dve.tensor_scalar(tmp[:, LAST, :], tmp[:, LAST, :], valid, None, ALU.mult))

                    def sum_nodes(v):
                        dve.tensor_reduce(g_sum[:, :], v[:, :, :].rearrange("p t f -> p f t"), AX.X,
                                          ALU.add).then_inc(sum_in, 1)

                    mask_pads()
                    sum_nodes(tmp)
                    sums += 1
                    dve.wait_ge(sum_out, sums)
                    chain(dve.tensor_scalar(g_a[:, :], ps_stat, -1.0 / N, None, ALU.mult))
                    chain(dve.tensor_tensor(g_a[:, :], g_a[:, :], scale, ALU.mult))
                    chain(dve.tensor_tensor(tmp[:, :, :], tmp[:, :, :], over_tiles(g_a[:, :]), ALU.add))
                    mask_pads()
                    chain(dve.tensor_tensor(agg[:, :, :], tmp[:, :, :], tmp[:, :, :], ALU.mult))
                    sum_nodes(agg)
                    sums += 1
                    dve.wait_ge(sum_out, sums)
                    roots += 1
                    dve.tensor_scalar(g_b[:, :], ps_stat, 1.0 / N, EPS, ALU.mult, ALU.add).then_inc(std_in, 1)
                    dve.wait_ge(std_out, roots)
                    chain(dve.reciprocal(g_b[:, :], g_b[:, :]))
                    chain(dve.tensor_tensor(g_b[:, :], g_b[:, :], w, ALU.mult))
                    chain(dve.tensor_tensor(tmp[:, :, :], tmp[:, :, :], over_tiles(g_b[:, :]), ALU.mult))
                    chain(dve.tensor_tensor(tmp[:, :, :], tmp[:, :, :], over_tiles(b), ALU.add))
                    last = dve.scalar_tensor_tensor(
                        out=h2[:, :, :], in0=tmp[:, :, :], scalar=0.0,
                        in1=node_tile[identity][:, :, :], op0=ALU.max, op1=ALU.add)
                    if to == "x":
                        chain(last)
                        last = dve.tensor_tensor(x[:, :, :], x[:, :, :], h2[:, :, :], ALU.add)
                    end_stage(last, i)

                elif stage[0] == "edges":
                    _, _, how, scale = stage
                    op0, op1 = (ALU.mult, ALU.add) if how == "sum" else (ALU.min, ALU.max)
                    if how == "max" and MAX_PASS[k] == 0:
                        for v in masks:
                            chain(dve.tensor_scalar(v, v, 2.0, -1.0, ALU.mult, ALU.add))
                            chain(dve.tensor_scalar(v, v, BIG, None, ALU.mult))
                    if how == "sum" and k and PASSES[k - 1][2] == "max":
                        for v in masks:
                            chain(dve.tensor_scalar(v, v, 0.0, None, ALU.is_gt))
                    for hf in range(2):
                        dve.tensor_copy(idx_stage[:, hf, :], src[:, hf * HALF:(hf + 1) * HALF]
                                        ).then_inc(idx_ready[hf], 1)
                    with dve.Fori(0, STEPS) as r:
                        chain.enter(r, 2 * HALF)
                        for hf in range(2):
                            chain(dve.tensor_copy(keep_stage[:, hf, :], keep[:, bass.ds(r * STEP + hf * HALF, HALF)]))
                            dve.wait_ge(gathered[k][hf], r * (16 * HALF) + 16 * HALF)
                            dve.tensor_copy(idx_stage[:, hf, :], src[:, bass.ds(r * STEP + STEP + hf * HALF, HALF)]
                                            ).then_inc(idx_ready[hf], 1)
                            if how == "max":
                                m = MAX_PASS[k]
                                dve.wait_ge(edge_ready[hf], r + STEPS * m + 2)
                                v = msg[:, hf, :, :].rearrange("p (g q) f -> p g (q f)", q=QUAD)
                                dve.tensor_tensor(v, v, ps_edge, ALU.add).then_inc(edge_used, 1)
                                dve.wait_ge(edge_used, r * 2 + 2 * STEPS * m + hf + 2)
                            dve.wait_ge(stored[hf], r * 16 + 16 * STEPS * k + 16)
                            prev = run[:, 1 - hf, HALF - 1, :]
                            for s in range(HALF):
                                last = dve.scalar_tensor_tensor(
                                    out=run[:, hf, s, :], in0=prev, scalar=keep_stage[:, hf, s:s + 1],
                                    in1=msg[:, hf, s, :], op0=op0, op1=op1)
                                prev = run[:, hf, s, :]
                                if s < HALF - 1:
                                    chain(last)
                            last.then_inc(scanned[hf], 1)
                            dve.wait_ge(scanned[hf], r + STEPS * k + 2)
                        chain.leave(STEPS)
                    dve.wait_ge(lastT_ready, k + 1)
                    dve.tensor_tensor_scan(chainT[:, 1:P + 1], crossT[:, :], ps_lastT, 0.0, op0, op1
                                           ).then_inc(chain_ready, 1)
                    dve.wait_ge(carry_ready, k + 1)
                    dve.wait_ge(row_gathered, 16 * (k + 1))
                    dve.scalar_tensor_tensor(out=fixed[:, :], in0=ps_carry, scalar=join, in1=fix_row[:, :],
                                             op0=op0, op1=op1).then_inc(row_fixed, 1)
                    dve.wait_ge(agg_gathered, 16 * TILES * (k + 1))
                    v = {"mean": mean_scale, "some": some}[scale]
                    end_stage(dve.tensor_tensor(agg[:, :, :], agg[:, :, :], over_features(v[:, :]), ALU.mult), i)


_INS = ["x", "src", "dst", "edge_attr_32", "L2_gnn_W1_edge", "L2_gnn_W2_edge"] + WEIGHTS + list(BIASES.values()) + NORMS


def kernel(**inputs):
    import numpy as np
    import concourse.bacc as bacc
    from concourse.bass_utils import run_bass_kernel_spmd

    nc = bacc.Bacc("TRN2", target_bir_lowering=False, num_devices=1)
    arrays, aps = {}, {}
    for name in _INS:
        v = np.ascontiguousarray(inputs[name])
        arrays[f"in_{name}"] = v
        aps[name] = nc.dram_tensor(f"in_{name}", v.shape, mybir.dt.from_np(v.dtype), kind="ExternalInput").ap()
    out = nc.dram_tensor("out", (N, D), mybir.dt.float32, kind="ExternalOutput").ap()
    build(nc, aps, out)
    r = run_bass_kernel_spmd(nc, [arrays], core_ids=[0])
    return r.results[0]["out"]
```

```python
from contextlib import ExitStack

import concourse.bass as bass
from concourse import mybir

P = 128
N, E, D, DE = 6250, 200000, 96, 32
TILES = -(-N // P)
NPAD = TILES * P
GROUP = 7
GROUPS = TILES // GROUP
HALF = 16
STEP = 2 * HALF
STEPS = -(-E // (P * STEP))
SLOTS = STEPS * STEP
TAIL = E - (P - 1) * SLOTS
MAIN, REST = 112, 15
QUAD = P // DE
BIG = 3.4028235e38
PAD_NODE = 8191
SRC_BITS = 13
WIN = 8
WINDOWS = NPAD // WIN
ROW = 32
ROWS = P * SLOTS // ROW
WIN_TILES = 3
WIN_ROWS = WIN_TILES * P // ROW
WIN_GROUP = 112
WIN_GROUPS = WINDOWS // WIN_GROUP
QUARTER = 4
CELLS = WIN * TILES
MAX_COUNT = 16.0
A_BUFS = 4
PARTS = 3
EPS = 1e-5

WEIGHTS = ["L0_gnn_W1_l", "L0_gnn_W1_r", "L0_gnn_W2_l", "L0_gnn_W2_r", "L1_gnn_W_self",
           "L1_gnn_W_neigh", "L2_gnn_W1_msg", "L2_gnn_W1_root", "L2_gnn_W2_msg",
           "L2_gnn_W2_root", "L3_gnn_W1", "L3_gnn_W2"]
BIASES = {"L0_gnn_W1_l": "L0_gnn_b1", "L0_gnn_W2_l": "L0_gnn_b2", "L1_gnn_W_self": "L1_gnn_b",
          "L2_gnn_W1_root": "L2_gnn_b1", "L2_gnn_W2_root": "L2_gnn_b2",
          "L3_gnn_W1": "L3_gnn_b1", "L3_gnn_W2": "L3_gnn_b2"}
NORMS = ["L3_gnn_gn1_w", "L3_gnn_gn1_b", "L3_gnn_gn1_a", "L3_gnn_gn2_w", "L3_gnn_gn2_b",
         "L3_gnn_gn2_a"]

STAGES = [
    ("setup",),
    ("norm",),
    ("edges", "h", "sum", "mean"),
    ("project", [("agg", "L0_gnn_W1_l"), ("h", "L0_gnn_W1_r")], "relu", "h2"),
    ("edges", "h2", "sum", "mean"),
    ("project", [("agg", "L0_gnn_W2_l"), ("h2", "L0_gnn_W2_r")], "add", "x"),
    ("norm",),
    ("edges", "h", "sum", "mean"),
    ("project", [("h", "L1_gnn_W_self"), ("agg", "L1_gnn_W_neigh")], "add", "x"),
    ("norm",),
    ("project", [("h", "L2_gnn_W1_msg")], "copy", "agg"),
    ("edges", "agg", "max", "some"),
    ("project", [("h", "L2_gnn_W1_root")], "leaky", "h2"),
    ("project", [("h2", "L2_gnn_W2_msg")], "copy", "agg"),
    ("edges", "agg", "max", "some"),
    ("project", [("h2", "L2_gnn_W2_root")], "leaky_add", "x"),
    ("norm",),
    ("edges", "h", "sum", "some"),
    ("project", [("agg", "L3_gnn_W1")], "copy", "agg2"),
    ("graphnorm", 0, "h", "h2"),
    ("edges", "h2", "sum", "some"),
    ("project", [("agg", "L3_gnn_W2")], "copy", "agg2"),
    ("graphnorm", 1, "h2", "x"),
]


def numbered():
    seen = {}
    for i, s in enumerate(STAGES):
        yield i, seen.get(s[0], 0), s
        seen[s[0]] = seen.get(s[0], 0) + 1


PASSES = [s for s in STAGES if s[0] == "edges"]
LOADS = 3 + 4 + len(WEIGHTS) + len(BIASES) + 2 * QUAD + len(NORMS)


class Chain:

    def __init__(self, engine, sem):
        self.engine, self.sem, self.n, self.reg, self.per = engine, sem, 0, None, 0

    def __call__(self, ins):
        self.n += 1
        ins.then_inc(self.sem, 1)
        self.engine.wait_ge(self.sem, self.n if self.reg is None else self.reg * self.per + self.n)

    def enter(self, reg, per):
        self.reg, self.per, self.at = reg, per, self.n

    def leave(self, trips):
        assert self.n == self.at + self.per
        self.n, self.reg = self.at + self.per * trips, None


def place(k):
    how = PASSES[k][2]
    return how, sum(s[2] == how for s in PASSES[:k])


def build(nc, a, out):
    f32, bf16, i32, f8 = mybir.dt.float32, mybir.dt.bfloat16, mybir.dt.int32, mybir.dt.float8e4
    ALU = mybir.AluOpType
    ACT = mybir.ActivationFunctionType
    AX = mybir.AxisListType

    with ExitStack() as ctx:
        def sb(name, shape, dt=f32):
            return ctx.enter_context(nc.sbuf_tensor(name, shape, dt))

        def sem(name):
            return ctx.enter_context(nc.semaphore(name))

        table = nc.dram_tensor("table", (NPAD, D), f32, kind="Internal").ap()
        running = nc.dram_tensor("running", (P * SLOTS, D), f32, kind="Internal").ap()
        keys = nc.dram_tensor("keys", (ROWS, ROW), i32, kind="Internal").ap()
        starts = nc.dram_tensor("starts", (NPAD + WIN,), i32, kind="Internal").ap()
        adjacency = nc.dram_tensor("adjacency", (TILES, P, TILES * P // 2), bf16, kind="Internal").ap()
        edge_tail = nc.dram_tensor("edge_tail", (SLOTS, DE), f32, kind="Internal").ap()

        x = sb("x_sb", [P, TILES, D])
        h = sb("h_sb", [P, TILES, D])
        h2 = sb("h2_sb", [P, TILES, D])
        agg = sb("agg_sb", [P, TILES, D])
        tmp = sb("tmp_sb", [P, TILES, D])
        node_tile = {"x": x, "h": h, "h2": h2, "agg": agg, "agg2": tmp}
        src = sb("src_sb", [P, SLOTS + STEP], i32)
        dst_f = sb("dst_f", [P, SLOTS])
        keep = sb("keep", [P, SLOTS])
        idx_stage = sb("idx_stage", [P, 2, HALF], i32)
        keep_stage = sb("keep_stage", [P, 2, HALF])
        edge_buf = sb("edge_buf", [P, 2 * HALF * (2 * D + DE)])
        msg = edge_buf[:, 0:2 * HALF * D].rearrange("p (b s f) -> p b s f", b=2, f=D)
        run = edge_buf[:, 2 * HALF * D:4 * HALF * D].rearrange("p (b s f) -> p b s f", b=2, f=D)
        ea = edge_buf[:, 4 * HALF * D:].rearrange("p (b s f) -> p b s f", b=2, f=DE)
        parts = edge_buf[:, 0:TILES * PARTS * D // 2].bitcast(bf16).rearrange("p (t k f) -> p t k f", k=PARTS, f=D)
        a_buf = sb("a_buf", [P, A_BUFS, TILES, P], f8)
        part_sum = sb("part_sum", [P, 2, D])
        eaT = sb("eaT", [P, 2, HALF // QUAD, P])
        fix_row = sb("fix_row", [P, D])
        fixed = sb("fixed", [P, D])
        chainT = sb("chainT", [D, P + 1])
        ident = sb("ident", [P, P])
        ones = sb("ones", [P, P])
        upto = sb("upto", [P, P])
        iota_i = sb("iota_i", [P, P], i32)
        iota_b = sb("iota_b", [P, P], bf16)
        zeros_b = sb("zeros_b", [P, P], bf16)
        over = sb("over", [P, 4 * TILES])
        neg_max = sb("neg_max", [P, 1])
        bad = sb("bad", [P, 2])
        ok_i = sb("ok_i", [P, 1], i32)
        edges_i = sb("edges_i", [1, 1], i32)
        win_i = sb("win_i", [WIN_GROUP, WIN_GROUPS], i32)
        start_w = sb("start_w", [WIN_GROUP, WIN_GROUPS], i32)
        next_w = sb("next_w", [WIN_GROUP, WIN_GROUPS], i32)
        row_w = sb("row_w", [WIN_GROUP, WIN_GROUPS], i32)
        need_w = sb("need_w", [WIN_GROUP, WIN_GROUPS])
        base_w = sb("base_w", [WIN_GROUP, WIN_GROUPS])
        ramp = sb("ramp", [WIN_GROUP, WIN_GROUPS, WIN_ROWS], i32)
        row_f = sb("row_f", [WIN_GROUP, WIN_GROUPS])
        ramp_f = sb("ramp_f", [WIN_GROUP, WIN_GROUPS, WIN_ROWS])
        rows_w = sb("rows_w", [WIN_GROUP, WIN_GROUPS, WIN_ROWS], i32)
        cols = sb("cols", [P, 2, WIN_TILES, P // WIN])
        start_n = sb("start_n", [P, TILES], i32)
        iota_c = sb("iota_c", [P, CELLS], mybir.dt.int16)

        def inside(tile, at, shape, dt):
            n = 1
            for v in shape[1:]:
                n *= v
            size = {f32: 4, i32: 4, bf16: 2, f8: 1}[dt]
            assert at * 4 + n * size <= TILES * D * 4 and n * size % 4 == 0
            v = tile[:, :, :].rearrange("p t f -> p (t f)")[0:shape[0], at:at + n * size // 4]
            v = v if dt == f32 else v.bitcast(dt)
            names = "abcd"[:len(shape) - 1]
            if len(names) == 1:
                return v
            return v.rearrange(f"p ({' '.join(names)}) -> p {' '.join(names)}",
                               **{c: m for c, m in zip(names, shape[1:])})

        dst_lo = inside(h2, 0, [P, SLOTS], bf16)
        dst_hi = inside(h2, SLOTS // 2, [P, SLOTS], bf16)
        key_i = inside(h2, SLOTS, [P, SLOTS], i32)
        lo_hot = inside(agg, 0, [P, 2, HALF, P], bf16)
        hi_hot = inside(agg, HALF * P, [P, 2, HALF, TILES], bf16)
        win_keys = inside(h, 0, [WIN_GROUP, 2, WIN_TILES * P], i32)
        win_tmp = inside(h, 2 * WIN_TILES * P, [WIN_GROUP, 2, WIN_TILES * P], i32)
        decoded = inside(agg, 0, [WIN_GROUP, 2, 2, WIN_TILES * P], f32)
        colsT = inside(h2, 0, [P, 2, WIN_TILES, WINDOWS], f32)
        cell_hot = inside(tmp, 0, [P, 2, QUARTER * WIN_TILES, CELLS], bf16)
        low_hot = inside(agg, 0, [P, 2, QUARTER * WIN_TILES, P], bf16)
        a_stage = inside(h, 0, [P, TILES, P], f8)
        junk = inside(agg, QUARTER * WIN_TILES * P, [P, 2, QUARTER * CELLS], f32)
        count = sb("count", [P, TILES])
        total = sb("total", [P, TILES])
        before = sb("before", [P, TILES])
        end_f = sb("end_f", [P, TILES])
        end_i = sb("end_i", [P, TILES], i32)
        some = sb("some", [P, TILES])
        mean_scale = sb("mean_scale", [P, TILES])
        stat = sb("stat", [P, 2, TILES])
        prev_i = sb("prev_i", [P, 1], i32)
        col = sb("col", [P, 8])
        first_i = sb("first_i", [P, 1], i32)
        start_i = sb("start_i", [P, 1], i32)
        wide = sb("wide", [P, D])
        crossT = sb("crossT", [D, P])
        w_all = sb("w_all", [D + 1, len(WEIGHTS), D])
        w_edge = sb("w_edge", [P, 2, QUAD, D])
        norm_p = sb("norm_p", [P, len(NORMS), D])
        node_stage = sb("node_stage", [P, 2, GROUP, D])
        nodeT = sb("nodeT", [D + 1, 2, GROUP, P])
        g_sum = sb("g_sum", [P, D])
        g_a = sb("g_a", [P, D])
        g_b = sb("g_b", [P, D])
        g_c = sb("g_c", [P, D])
        ps = ctx.enter_context(nc.psum_tensor("ps", [P, 8, 512], f32))

        ps_nodeT = [ps[0:D, 2 * i:2 * i + 2, :].rearrange("p b (t n) -> p (b t) n", n=P)[:, 0:GROUP, :]
                    for i in range(2)]
        ps_out = ps[:, 4:6, :].rearrange("p b (t n) -> p (b t) n", n=P)[:, 0:GROUP, 0:D]
        ps_outw = ps[:, 4:6, :].rearrange("p b (t n) -> p (b t) n", n=P)
        ps_eaT = [ps[:, i, :].rearrange("p (q n) -> p q n", n=P) for i in range(2)]
        ps_edge = ps[:, 2:6, 0:QUAD * D]
        ps_dec = ps[:, 0:4, 0:WIN_TILES * WIN_GROUP].rearrange("p (b v) (k n) -> p b v k n", v=2, n=WIN_GROUP)
        ps_cells = ps[:, :, 0:CELLS].rearrange("p (b w) c -> p b w c", b=2)
        ps_acc = ps[:, 0:2, 0:PARTS * D]
        ps_bad = ps[:, 7, 0:1]
        ps_count = ps[:, 6, 0:TILES]
        ps_cum = ps[:, 6, 64:64 + TILES]
        ps_tot = ps[:, 6, 128:128 + TILES]
        ps_lastT = ps[0:D, 7, 0:P]
        ps_carry = ps[:, 7, 128:128 + D]
        ps_stat = ps[:, 7, 256:256 + D]

        stage_done = sem("stage_done")
        dve_done = sem("dve_done")
        loaded = sem("loaded")
        dst_loaded = sem("dst_loaded")
        zeroed = sem("zeroed")
        ready = sem("constants_ready")
        pool_made = sem("pool_made")
        hot_ready = sem("hot_ready")
        hot_used = sem("hot_used")
        count_ready = sem("count_ready")
        count_copied = sem("count_copied")
        cum_ready = sem("cum_ready")
        wide_ready = sem("wide_ready")
        wideT_ready = sem("wideT_ready")
        staged = sem("staged")
        transposed = sem("transposed")
        lhs_ready = sem("lhs_ready")
        projected = sem("projected")
        drained = sem("drained")
        std_in = sem("std_in")
        std_out = sem("std_out")
        sum_in = sem("sum_in")
        sum_out = sem("sum_out")
        def edge_set(name, passes):
            return dict(
                steps=sem(f"{name}_steps"),
                table_stored=sem(f"{name}_table_stored"),
                idx_ready=[sem(f"{name}_idx_ready{i}") for i in range(2)],
                gathered=[[sem(f"{name}_gathered{n}_{i}") for i in range(2)] for n in range(passes)],
                scanned=[sem(f"{name}_scanned{i}") for i in range(2)],
                stored=[sem(f"{name}_stored{i}") for i in range(2)],
                lastT_ready=sem(f"{name}_lastT_ready"),
                chain_ready=sem(f"{name}_chain_ready"),
                carry_ready=sem(f"{name}_carry_ready"),
                row_gathered=sem(f"{name}_row_gathered"),
                row_fixed=sem(f"{name}_row_fixed"),
                row_stored=sem(f"{name}_row_stored"),
                agg_gathered=sem(f"{name}_agg_gathered"))

        sets = {"sum": edge_set("sum", 5), "max": edge_set("max", 2)}
        ea_loaded = [sem(f"ea_loaded{i}") for i in range(2)]
        ea_turned = [sem(f"ea_turned{i}") for i in range(2)]
        eaT_ready = [sem(f"eaT_ready{i}") for i in range(2)]
        edge_ready = [sem(f"edge_ready{i}") for i in range(2)]
        edge_used = sem("edge_used")
        keys_made = sem("keys_made")
        keys_stored = sem("keys_stored")
        starts_made = sem("starts_made")
        starts_stored = sem("starts_stored")
        starts_loaded = sem("starts_loaded")
        rows_ready = sem("rows_ready")
        win_gathered = [sem(f"win_gathered{i}") for i in range(2)]
        decoded_ready = sem("decoded_ready")
        dec_turned = sem("dec_turned")
        colsT_ready = sem("colsT_ready")
        build_hot = sem("build_hot")
        cells_ready = sem("cells_ready")
        cells_copied = sem("cells_copied")
        block_stored = sem("block_stored")
        stage_free = sem("stage_free")
        bad_ready = sem("bad_ready")
        bad_summed = sem("bad_summed")
        ok_ready = sem("ok_ready")
        dense_steps = sem("dense_steps")
        parts_ready = sem("parts_ready")
        a_loaded = [sem(f"a_loaded{i}") for i in range(A_BUFS)]
        a_used = [sem(f"a_used{i}") for i in range(A_BUFS)]
        acc_used = sem("acc_used")
        out_stored = sem("out_stored")
        marks = sem("marks")

        EDGE_PARTS = [(0, MAIN), (MAIN, P - 1), (P - 1, P)]

        def by_tile(v):
            return v.rearrange("(t p) f -> p t f", p=P)

        running_rows = running.rearrange("(p s) f -> p (s f)", p=P)
        dst_i = tmp[:, :, :].bitcast(i32).rearrange("p t f -> p (t f)")[:, 0:SLOTS]
        part_i = agg[:, :, :].bitcast(i32).rearrange("p t f -> p (t f)")[:, 0:SLOTS]
        scratch = h[:, :, :].rearrange("p t f -> p (t f)")[:, 0:SLOTS]
        valid, prev_f, join, full, cross, first_n, first_f, start_f = (col[:, i:i + 1] for i in range(8))
        LAST = TILES - 1
        LAST_N = N - LAST * P

        block = ctx.enter_context(nc.Block())

        @block.sync
        def _(sp):
            def load_edges(to, v, done):
                for p0, p1 in EDGE_PARTS:
                    part = v[p0 * SLOTS:min(p1 * SLOTS, E)]
                    w = part.shape[0] // (p1 - p0)
                    sp.dma_start(to[p0:p1, 0:w], part.rearrange("(p s) -> p s", s=w)).then_inc(done, 16)

            def store_running(r, hf, q, n):
                sp.wait_ge(q["scanned"][hf], r + STEPS * n + 2)
                sp.dma_start(running_rows[:, bass.ds(r * (STEP * D) + hf * HALF * D, HALF * D)],
                             run[:, hf, :, :].rearrange("p s f -> p (s f)")).then_inc(q["stored"][hf], 16)

            def load_attributes(r, hf):
                at = bass.ds(r * (STEP * DE) + hf * HALF * DE, HALF * DE)
                for p0, p1 in EDGE_PARTS:
                    v = a["edge_attr_32"][p0 * SLOTS:p1 * SLOTS, :] if p1 < P else edge_tail
                    sp.dma_start(ea[p0:p1, hf, :, :].rearrange("p s f -> p (s f)"),
                                 v.rearrange("(p s) f -> p (s f)", s=SLOTS)[:, at]).then_inc(ea_loaded[hf], 16)

            sp.sem_inc(stage_free, 1)
            sp.wait_ge(zeroed, 1)
            for i, q in enumerate(sets.values()):
                for hf in range(2):
                    sp.dma_start(running_rows[:, (2 * i + hf) * HALF * D:(2 * i + hf + 1) * HALF * D],
                                 run[:, hf, :, :].rearrange("p s f -> p (s f)")).then_inc(q["stored"][hf], 16)
            load_edges(dst_i, a["dst"], dst_loaded)
            with nc.allow_non_contiguous_dma(reason="one word for each partition"):
                sp.dma_start(prev_i[1:P, :], a["dst"][SLOTS - 1:(P - 1) * SLOTS:SLOTS].unsqueeze(1)
                             ).then_inc(dst_loaded, 16)
            load_edges(src, a["src"], loaded)
            sp.dma_start(x[:, 0:LAST, :], by_tile(a["x"][0:LAST * P, :])).then_inc(loaded, 16)
            sp.dma_start(x[0:LAST_N, LAST, :], a["x"][LAST * P:N, :]).then_inc(loaded, 16)
            sp.dma_start(edge_tail[0:TAIL, :], a["edge_attr_32"][E - TAIL:E, :]).then_inc(loaded, 16)
            sp.dma_start(edge_tail[TAIL:SLOTS, :].rearrange("(p q) f -> p (q f)", p=64),
                         run[0:64, :, :, :].rearrange("p a s f -> p (a s f)")[:, 0:(SLOTS - TAIL) * DE // 64]
                         ).then_inc(loaded, 16)
            for i, name in enumerate(WEIGHTS):
                sp.dma_start(w_all[0:D, i, :], a[name]).then_inc(loaded, 16)
                if name in BIASES:
                    sp.dma_start(w_all[D:D + 1, i, :], a[BIASES[name]].unsqueeze(0)).then_inc(loaded, 16)
            for i, name in enumerate(("L2_gnn_W1_edge", "L2_gnn_W2_edge")):
                for q in range(QUAD):
                    sp.dma_start(w_edge[q * DE:(q + 1) * DE, i, q, :], a[name]).then_inc(loaded, 16)
            for i, name in enumerate(NORMS):
                sp.dma_start(norm_p[:, i, :], a[name].unsqueeze(0).to_broadcast([P, D])).then_inc(loaded, 16)

            sp.wait_ge(keys_made, 1)
            sp.dma_start(keys.rearrange("(p r) c -> p (r c)", p=P), key_i).then_inc(keys_stored, 16)
            sp.wait_ge(starts_made, 1)
            with nc.allow_non_contiguous_dma(reason="single words: one for each node"):
                sp.dma_start(starts[0:NPAD].rearrange("(t p) -> p t", p=P), start_n[:, :]).then_inc(starts_stored, 16)
                sp.dma_start(starts[NPAD:NPAD + 1].unsqueeze(0), edges_i[:, :]).then_inc(starts_stored, 16)
                sp.wait_ge(starts_stored, 32)
                for to, first in ((start_w, 0), (next_w, WIN)):
                    sp.dma_start(to[:, :], starts[first:first + NPAD].rearrange("(g w e) -> w g e", w=WIN_GROUP, e=WIN)
                                 [:, :, 0]).then_inc(starts_loaded, 16)
            with sp.Fori(0, TILES) as r:
                sp.wait_ge(cells_copied, r * 4 + 4 + 2)
                sp.sem_inc(marks, 1)
                sp.dma_start(adjacency[bass.ds(r, 1), :, :].rearrange("a p n -> (a p) n"),
                             a_stage.rearrange("p t n -> p (t n)").bitcast(bf16)).then_inc(block_stored, 16)
                sp.wait_ge(block_stored, r * 16 + 16)
                sp.sem_inc(stage_free, 1)

            sp.wait_ge(ok_ready, 1)
            dense = sp.value_load(ok_i[0:1, 0:1], min_val=0, max_val=1)
            for i, k, stage in numbered():
                if stage[0] != "edges":
                    continue
                how, n = place(k)
                q = sets[how]
                if how == "sum":
                    with sp.If(dense):
                        with sp.Fori(0, GROUPS) as r:
                            for b in range(GROUP):
                                uses = len(range(b % A_BUFS, GROUP, A_BUFS))
                                sp.wait_ge(a_used[b % A_BUFS], r * uses + uses * GROUPS * n + b // A_BUFS + 1)
                                sp.dma_start(a_buf[:, b % A_BUFS, :, :].rearrange("p t n -> p (t n)").bitcast(bf16),
                                             adjacency[bass.ds(r * GROUP + b, 1), :, :].rearrange("a p n -> (a p) n")
                                             ).then_inc(a_loaded[b % A_BUFS], 16)
                    with sp.Else():
                        sp.wait_ge(stage_done, i)
                        sp.dma_start(by_tile(table), node_tile[stage[1]][:, :, :]).then_inc(q["table_stored"], 16)
                        with sp.Fori(0, STEPS) as r:
                            for hf in range(2):
                                store_running(r, hf, q, n)
                else:
                    sp.wait_ge(stage_done, i)
                    sp.dma_start(by_tile(table), node_tile[stage[1]][:, :, :]).then_inc(q["table_stored"], 16)
                    for hf in range(2):
                        load_attributes(0, hf)
                    with sp.Fori(0, STEPS - 1) as r:
                        for hf in range(2):
                            store_running(r, hf, q, n)
                            sp.wait_ge(ea_turned[hf], r + STEPS * n + 1)
                            load_attributes(r + 1, hf)
                    for hf in range(2):
                        store_running(STEPS - 1, hf, q, n)
            sp.wait_ge(stage_done, len(STAGES))
            sp.dma_start(by_tile(out[0:LAST * P, :]), x[:, 0:LAST, :]).then_inc(out_stored, 16)
            sp.dma_start(out[LAST * P:N, :], x[0:LAST_N, LAST, :]).then_inc(out_stored, 16)
            sp.wait_ge(out_stored, 32)

        @block.gpsimd
        def _(pool):
            pool.memset(ident[:, :], 0.0)
            pool.memset(upto[:, :], 1.0).then_inc(pool_made, 1)
            pool.wait_ge(pool_made, 1)
            pool.affine_select(out=ident[:, :], in_=ident[:, :], compare_op=ALU.not_equal, fill=1.0,
                               base=0, pattern=[[-1, P]], channel_multiplier=1)
            pool.affine_select(out=upto[:, :], in_=upto[:, :], compare_op=ALU.is_ge, fill=0.0,
                               base=0, pattern=[[1, P]], channel_multiplier=-1)
            pool.iota(iota_i[:, :], pattern=[[1, P]], base=0, channel_multiplier=0)
            pool.iota(iota_c[:, :], pattern=[[1, CELLS]], base=0, channel_multiplier=0)
            pool.iota(win_i[:, :], pattern=[[WIN_GROUP, WIN_GROUPS]], base=0, channel_multiplier=1)
            pool.iota(ramp[:, :, :], pattern=[[0, WIN_GROUPS], [1, WIN_ROWS]], base=0, channel_multiplier=0)
            pool.iota(start_i[:, :], pattern=[[0, 1]], base=0, channel_multiplier=SLOTS).then_inc(ready, 1)

            def gather(to, frm, idx, done):
                pool.indirect_dma_start(to, None, frm, bass.IndirectOffsetOnAxis(ap=idx, axis=0)
                                        ).then_inc(done, 16)

            pool.wait_ge(rows_ready, 1)
            pool.wait_ge(keys_stored, 16)
            for g in range(WIN_GROUPS):
                if g >= 2:
                    pool.wait_ge(decoded_ready, g - 1)
                for row in range(WIN_ROWS):
                    gather(win_keys[:, g % 2, row * ROW:(row + 1) * ROW], keys, rows_w[:, g, row:row + 1],
                           win_gathered[g % 2])

            def edge_pass(q, n):
                with pool.Fori(0, STEPS) as r:
                    for hf in range(2):
                        pool.wait_ge(q["table_stored"], 16 * (n + 1))
                        pool.wait_ge(q["idx_ready"][hf], r + (STEPS + 1) * n + 1)
                        pool.wait_ge(q["scanned"][hf], r + STEPS * n + 1)
                        pool.sem_inc(marks, 1)
                        for s in range(HALF):
                            gather(msg[:, hf, s, :], table, idx_stage[:, hf, s:s + 1], q["gathered"][n][hf])
                for hf in range(2):
                    pool.wait_ge(q["stored"][hf], 16 * STEPS * (n + 1) + 16)
                gather(fix_row[:, :], running, first_i[:, :], q["row_gathered"])
                pool.wait_ge(q["row_fixed"], n + 1)
                pool.indirect_dma_start(running, bass.IndirectOffsetOnAxis(ap=first_i[:, :], axis=0),
                                        fixed[:, :], None).then_inc(q["row_stored"], 16)
                pool.wait_ge(q["row_stored"], 16 * (n + 1))
                for t in range(TILES):
                    gather(agg[:, t, :], running, end_i[:, t:t + 1], q["agg_gathered"])

            pool.wait_ge(ok_ready, 1)
            dense = pool.value_load(ok_i[0:1, 0:1], min_val=0, max_val=1)
            for i, k, stage in numbered():
                if stage[0] != "edges":
                    continue
                how, n = place(k)
                if how == "max":
                    edge_pass(sets[how], n)
                else:
                    with pool.If(1 - dense):
                        edge_pass(sets[how], n)

        @block.scalar
        def _(act):
            for s in (lhs_ready, *eaT_ready):
                act.sem_inc(s, 1)
            act.sem_inc(cells_copied, 2)
            for g in range(WIN_GROUPS):
                act.wait_ge(dec_turned, g + 1)
                act.copy(colsT[:, :, :, g * WIN_GROUP:(g + 1) * WIN_GROUP], ps_dec[:, g % 2, :, :, :]
                         ).then_inc(colsT_ready, 1)
            with act.Fori(0, TILES) as r:
                act.wait_ge(stage_free, r + 1)
                for c in range(4):
                    cells = ps_cells[:, c % 2, :, :]
                    act.wait_ge(cells_ready, r * 4 + c + 3)
                    act.activation(junk[:, c % 2, :].rearrange("p (w c) -> p w c", c=CELLS), cells, ACT.Relu,
                                   bias=neg_max[:, :], accum_out=over[:, bass.ds(r * 4 + c, 1)])
                    act.copy(a_stage[:, :, c * 32:(c + 1) * 32].rearrange("p t (w d) -> p w d t", d=WIN),
                             cells.rearrange("p w (d t) -> p w d t", t=TILES), saturate=False
                             ).then_inc(cells_copied, 1)
            roots = 0
            for i, k, stage in numbered():
                act.wait_ge(stage_done, i)
                if stage[0] in ("norm", "graphnorm"):
                    roots += 1
                    v = stat[:, 1, :] if stage[0] == "norm" else g_b[:, :]
                    act.wait_ge(std_in, roots)
                    act.activation(v, v, ACT.Sqrt).then_inc(std_out, 1)
                elif stage[0] == "project":
                    n = len(stage[1])
                    with act.Fori(0, GROUPS) as r:
                        act.wait_ge(transposed, r + GROUPS * k + 1)
                        for j, (name, _) in enumerate(stage[1]):
                            last = act.copy(node_stage[:, j, :, :],
                                            node_tile[name][:, bass.ds(r * GROUP, GROUP), :])
                        last.then_inc(staged, 1)
                        act.wait_ge(transposed, r + GROUPS * k + 2)
                        act.wait_ge(projected, r + GROUPS * k + 1)
                        for j in range(n):
                            last = act.copy(nodeT[0:D, j, :, :], ps_nodeT[j])
                        last.then_inc(lhs_ready, 1)
                elif stage[0] == "edges" and stage[2] == "max":
                    m = place(k)[1]
                    with act.Fori(0, STEPS) as r:
                        for hf in range(2):
                            act.wait_ge(ea_turned[hf], r + STEPS * m + 1)
                            act.wait_ge(edge_ready[hf], r + STEPS * m + 1)
                            act.copy(eaT[:, hf, :, :], ps_eaT[hf]).then_inc(eaT_ready[hf], 1)

        @block.tensor
        def _(pe):
            for s in (transposed, projected, hot_used, *edge_ready, *a_used):
                pe.sem_inc(s, 1)
            pe.sem_inc(cells_ready, 2)
            pe.wait_ge(ready, 1)
            pe.wait_ge(zeroed, 1)
            pe.matmul(ps_count, zeros_b[:, :], zeros_b[:, 0:TILES], start=True, stop=False)
            with pe.Fori(0, STEPS) as r:
                for hf in range(2):
                    pe.wait_ge(hot_ready, r * 2 + hf + 1)
                    for s in range(HALF):
                        last = pe.matmul(ps_count, lo_hot[:, hf, s, :], hi_hot[:, hf, s, :],
                                         start=False, stop=False)
                    last.then_inc(hot_used, 1)
            pe.matmul(ps_count, zeros_b[:, :], zeros_b[:, 0:TILES], start=False, stop=True).then_inc(count_ready, 1)
            pe.wait_ge(count_copied, 1)
            pe.matmul(ps_cum, upto[:, :], count[:, :], start=True, stop=True)
            pe.matmul(ps_tot, ones[:, :], count[:, :], start=True, stop=True).then_inc(cum_ready, 1)
            pe.wait_ge(wide_ready, 1)
            pe.transpose(ps_lastT, wide[:, :], ident[:, :]).then_inc(wideT_ready, 1)
            for g in range(WIN_GROUPS):
                pe.wait_ge(decoded_ready, g + 1)
                if g >= 2:
                    pe.wait_ge(colsT_ready, g - 1)
                for v in range(2):
                    for j in range(WIN_TILES):
                        last = pe.transpose(ps_dec[:, g % 2, v, j, :], decoded[:, g % 2, v, j * P:(j + 1) * P],
                                            ident[0:WIN_GROUP, 0:WIN_GROUP])
                last.then_inc(dec_turned, 1)
            pe.wait_ge(colsT_ready, WIN_GROUPS)
            with pe.Fori(0, TILES) as r:
                for c in range(4):
                    pe.wait_ge(build_hot, r * 4 + c + 2)
                    pe.wait_ge(cells_copied, r * 4 + c + 1)
                    for w in range(QUARTER):
                        for j in range(WIN_TILES):
                            m = j * QUARTER + w
                            last = pe.matmul(ps_cells[:, c % 2, w, :], low_hot[:, c % 2, m, :],
                                             cell_hot[:, c % 2, m, :], start=(j == 0), stop=(j == WIN_TILES - 1))
                    last.then_inc(cells_ready, 1)
            pe.wait_ge(bad_ready, 1)
            pe.matmul(ps_bad, ones[:, :], bad[:, 0:1], start=True, stop=True).then_inc(bad_summed, 1)
            pe.wait_ge(ok_ready, 1)
            dense = pe.value_load(ok_i[0:1, 0:1], min_val=0, max_val=1)

            def dense_pass(n):
                pe.wait_ge(parts_ready, n + 1)
                with pe.Fori(0, GROUPS) as r:
                    for b in range(GROUP):
                        buf = b % A_BUFS
                        uses = len(range(buf, GROUP, A_BUFS))
                        pe.wait_ge(a_loaded[buf], r * (16 * uses) + 16 * (uses * GROUPS * n + b // A_BUFS + 1))
                        pe.wait_ge(acc_used, r * GROUP + TILES * n + b + 1)
                        pe.sem_inc(marks, 1)
                        for t in range(TILES):
                            last = pe.matmul(ps[:, b, 0:PARTS * D], a_buf[:, buf, t, :],
                                             parts[:, t, :, :].rearrange("p k f -> p (k f)"),
                                             start=(t == 0), stop=(t == TILES - 1))
                        last.then_inc(a_used[buf], 1)

            def mend(q, n):
                pe.wait_ge(q["scanned"][1], STEPS * (n + 1) + 1)
                pe.transpose(ps_lastT, run[:, 1, HALF - 1, :], ident[:, :]).then_inc(q["lastT_ready"], 1)
                pe.wait_ge(q["chain_ready"], n + 1)
                pe.transpose(ps_carry, chainT[:, 0:P], ident[0:D, 0:D]).then_inc(q["carry_ready"], 1)

            sums = 0
            for i, k, stage in numbered():
                pe.wait_ge(stage_done, i)
                if stage[0] == "graphnorm":
                    for _ in range(2):
                        sums += 1
                        pe.wait_ge(sum_in, sums)
                        pe.matmul(ps_stat, ones[:, :], g_sum[:, :], start=True, stop=True).then_inc(sum_out, 1)
                elif stage[0] == "project":
                    n = len(stage[1])
                    with pe.Fori(0, GROUPS) as r:
                        pe.wait_ge(staged, r + GROUPS * k + 1)
                        pe.wait_ge(lhs_ready, r + GROUPS * k + 1)
                        for j in range(n):
                            for t in range(GROUP):
                                last = pe.transpose(ps_nodeT[j][:, t, :], node_stage[:, j, t, :], ident[:, :])
                        last.then_inc(transposed, 1)
                        pe.wait_ge(lhs_ready, r + GROUPS * k + 2)
                        pe.wait_ge(drained, r + GROUPS * k + 1)
                        for t in range(GROUP):
                            for j, (_, w) in enumerate(stage[1]):
                                last = pe.matmul(ps_out[:, t, :], nodeT[:, j, t, :], w_all[:, WEIGHTS.index(w), :],
                                                 start=(j == 0), stop=(j == n - 1))
                        last.then_inc(projected, 1)
                elif stage[0] == "edges":
                    how, m = place(k)
                    if how == "sum":
                        with pe.If(dense):
                            dense_pass(m)
                        with pe.Else():
                            mend(sets[how], m)
                    else:
                        with pe.Fori(0, STEPS) as r:
                            for hf in range(2):
                                pe.wait_ge(ea_loaded[hf], r * 48 + 48 * (STEPS * m + 1))
                                pe.wait_ge(eaT_ready[hf], r + STEPS * m + 1)
                                for g in range(HALF // QUAD):
                                    last = pe.transpose(ps_eaT[hf][:, g, :],
                                                        ea[:, hf, g * QUAD:(g + 1) * QUAD, :].rearrange("p s f -> p (s f)"),
                                                        ident[:, :])
                                last.then_inc(ea_turned[hf], 1)
                                pe.wait_ge(eaT_ready[hf], r + STEPS * m + 2)
                                pe.wait_ge(edge_used, r * 2 + 2 * STEPS * m + hf + 1)
                                for g in range(HALF // QUAD):
                                    last = pe.matmul(ps_edge[:, g, :], eaT[:, hf, g, :],
                                                     w_edge[:, m, :, :].rearrange("p q f -> p (q f)"),
                                                     start=True, stop=True)
                                last.then_inc(edge_ready[hf], 1)
                        mend(sets[how], m)

        @block.vector
        def _(dve):
            chain = Chain(dve, dve_done)
            gather_chain = {how: Chain(dve, q["steps"]) for how, q in sets.items()}
            dense_chain = Chain(dve, dense_steps)
            for s in (drained, edge_used, *sets["sum"]["scanned"], *sets["max"]["scanned"]):
                dve.sem_inc(s, 1)
            dve.sem_inc(acc_used, GROUP)
            dve.sem_inc(build_hot, 1)

            def end_stage(ins, i):
                ins.then_inc(stage_done, 1)
                dve.wait_ge(stage_done, i + 1)

            def over_tiles(v):
                return v.unsqueeze(1).to_broadcast([P, TILES, D])

            def over_features(v):
                return v.unsqueeze(2).to_broadcast([P, TILES, D])

            for v, value in ((src, 0), (dst_i, PAD_NODE), (prev_i, -1), (zeros_b, 0.0), (ones, 1.0),
                             (w_edge, 0.0), (w_all[D:D + 1, :, :], 0.0), (nodeT[D:D + 1, :, :, :], 1.0),
                             (chainT[:, 0:1], 0.0), (edge_buf, 0.0), (bad, 0.0), (neg_max, -MAX_COUNT), (edges_i, E), (x[:, LAST, :], 0.0), (keep[:, 0:1], 0.0)):
                last = dve.memset(v if isinstance(v, bass.AP) else v[tuple(slice(None) for _ in v.shape)], value)
            last.then_inc(zeroed, 1)
            dve.wait_ge(zeroed, 1)
            dve.wait_ge(ready, 1)
            chain(dve.tensor_copy(iota_b[:, :], iota_i[:, :]))
            dve.wait_ge(dst_loaded, 64)
            chain(dve.tensor_copy(dst_f[:, :], dst_i))
            dve.wait_ge(loaded, 16 * LOADS)
            chain(dve.tensor_scalar(part_i, dst_i, SRC_BITS, None, ALU.logical_shift_left))
            dve.tensor_tensor(key_i, part_i, src[:, 0:SLOTS], ALU.bitwise_or).then_inc(keys_made, 1)
            dve.wait_ge(keys_made, 1)
            chain(dve.tensor_scalar(part_i, dst_i, 7, None, ALU.arith_shift_right))
            chain(dve.tensor_copy(dst_hi[:, :], part_i))
            chain(dve.tensor_scalar(part_i, dst_i, P - 1, None, ALU.bitwise_and))
            chain(dve.tensor_copy(dst_lo[:, :], part_i))
            chain(dve.tensor_tensor(keep[:, 1:SLOTS], dst_f[:, 1:SLOTS], dst_f[:, 0:SLOTS - 1], ALU.is_equal))
            chain(dve.tensor_copy(start_f, start_i[:, :]))
            chain(dve.tensor_scalar(valid, start_f, float(LAST_N * SLOTS), None, ALU.is_lt))
            chain(dve.tensor_copy(prev_f, prev_i[:, :]))
            chain(dve.tensor_tensor(join, dst_f[:, 0:1], prev_f, ALU.is_equal))
            chain(dve.tensor_tensor(full, dst_f[:, 0:1], dst_f[:, SLOTS - 1:SLOTS], ALU.is_equal))
            chain(dve.tensor_tensor(cross, join, full, ALU.mult))
            chain(dve.tensor_scalar(scratch, dst_f[:, :], dst_f[:, 0:1], None, ALU.is_equal, ALU.add,
                                    accum_out=first_n))
            chain(dve.tensor_tensor(first_f, start_f, first_n, ALU.add))
            chain(dve.tensor_scalar(first_f, first_f, -1.0, None, ALU.add))
            chain(dve.tensor_copy(first_i[:, :], first_f))
            dve.tensor_copy(wide[:, :], cross.to_broadcast([P, D])).then_inc(wide_ready, 1)
            with dve.Fori(0, STEPS) as r:
                for hf in range(2):
                    at = bass.ds(r * STEP + hf * HALF, HALF)
                    if hf == 0:
                        dve.wait_ge(hot_used, r * 2 + 1)
                    dve.tensor_tensor(lo_hot[:, hf, :, :], iota_b[:, :].unsqueeze(1).to_broadcast([P, HALF, P]),
                                      dst_lo[:, at].unsqueeze(2).to_broadcast([P, HALF, P]), ALU.is_equal)
                    dve.tensor_tensor(hi_hot[:, hf, :, :],
                                      iota_b[:, 0:TILES].unsqueeze(1).to_broadcast([P, HALF, TILES]),
                                      dst_hi[:, at].unsqueeze(2).to_broadcast([P, HALF, TILES]), ALU.is_equal
                                      ).then_inc(hot_ready, 1)
            dve.wait_ge(count_ready, 1)
            dve.tensor_copy(count[:, :], ps_count).then_inc(count_copied, 1)
            dve.wait_ge(count_copied, 1)
            dve.wait_ge(cum_ready, 1)
            chain(dve.tensor_copy(total[:, :], ps_tot))
            chain(dve.tensor_tensor_scan(before[:, :], ones[:, 0:TILES], total[:, :], 0.0, ALU.mult, ALU.add))
            chain(dve.tensor_tensor(before[:, :], before[:, :], total[:, :], ALU.subtract))
            chain(dve.tensor_tensor(end_f[:, :], before[:, :], ps_cum, ALU.add))
            chain(dve.tensor_scalar(end_f[:, :], end_f[:, :], -1.0, 0.0, ALU.add, ALU.max))
            chain(dve.tensor_copy(end_i[:, :], end_f[:, :]))
            chain(dve.tensor_scalar(some[:, :], count[:, :], 0.0, None, ALU.is_gt))
            chain(dve.tensor_scalar(mean_scale[:, :], count[:, :], 1.0, None, ALU.max))
            chain(dve.reciprocal(mean_scale[:, :], mean_scale[:, :]))
            chain(dve.tensor_tensor(mean_scale[:, :], mean_scale[:, :], some[:, :], ALU.mult))
            dve.wait_ge(wideT_ready, 1)
            chain(dve.tensor_copy(crossT[:, :], ps_lastT))

            chain(dve.tensor_tensor(before[:, :], before[:, :], ps_cum, ALU.add))
            chain(dve.tensor_tensor(before[:, :], before[:, :], count[:, :], ALU.subtract))
            dve.tensor_copy(start_n[:, :], before[:, :]).then_inc(starts_made, 1)
            dve.wait_ge(starts_loaded, 32)
            chain(dve.tensor_scalar(row_w[:, :], start_w[:, :], 5, None, ALU.arith_shift_right))
            chain(dve.tensor_copy(row_f[:, :], row_w[:, :]))
            chain(dve.tensor_copy(ramp_f[:, :, :], ramp[:, :, :]))
            dve.tensor_tensor(rows_w[:, :, :], ramp_f[:, :, :],
                              row_f[:, :].unsqueeze(2).to_broadcast([WIN_GROUP, WIN_GROUPS, WIN_ROWS]), ALU.add
                              ).then_inc(rows_ready, 1)
            chain(dve.scalar_tensor_tensor(out=need_w[:, :], in0=row_w[:, :], scalar=-float(ROW), in1=next_w[:, :],
                                           op0=ALU.mult, op1=ALU.add))
            chain(dve.tensor_scalar(need_w[:, :], need_w[:, :], float(WIN_TILES * P), None, ALU.is_gt))
            chain(dve.tensor_reduce(bad[0:WIN_GROUP, 0:1], need_w[:, :], AX.X, ALU.max))
            chain(dve.tensor_scalar(base_w[:, :], win_i[:, :], -float(CELLS), None, ALU.mult))
            for g in range(WIN_GROUPS):
                par = g % 2
                d, t = win_tmp[:, 0, :], win_tmp[:, 1, :]
                dve.wait_ge(win_gathered[par], 16 * WIN_ROWS * (g // 2 + 1))
                key = win_keys[:, par, :]
                chain(dve.tensor_scalar(d, key, SRC_BITS, None, ALU.logical_shift_right))
                chain(dve.tensor_scalar(t, key, 7, 63, ALU.logical_shift_right, ALU.bitwise_and))
                if g >= 2:
                    dve.wait_ge(dec_turned, g - 1)
                chain(dve.scalar_tensor_tensor(out=decoded[:, par, 0, :], in0=d, scalar=float(TILES), in1=t,
                                               op0=ALU.mult, op1=ALU.add))
                chain(dve.tensor_scalar(decoded[:, par, 0, :], decoded[:, par, 0, :], base_w[:, g:g + 1], None,
                                        ALU.add))
                chain(dve.tensor_scalar(d, key, P - 1, None, ALU.bitwise_and))
                dve.tensor_copy(decoded[:, par, 1, :], d).then_inc(decoded_ready, 1)
                dve.wait_ge(decoded_ready, g + 1)
            dve.wait_ge(colsT_ready, WIN_GROUPS)
            with dve.Fori(0, TILES) as r:
                chain.enter(r, 1)
                dve.wait_ge(build_hot, r * 4 + 1)
                chain(dve.tensor_copy(cols[:, :, :, :], colsT[:, :, :, bass.ds(r * (P // WIN), P // WIN)]))
                for c in range(4):
                    dve.wait_ge(cells_ready, r * 4 + c + 1)
                    for j in range(WIN_TILES):
                        for w in range(QUARTER):
                            dve.tensor_scalar(cell_hot[:, c % 2, j * QUARTER + w, :], iota_c[:, :],
                                              cols[:, 0, j, c * QUARTER + w:c * QUARTER + w + 1], None, ALU.is_equal)
                    dve.tensor_tensor(
                        low_hot[:, c % 2, :, :].rearrange("p (j w) n -> p j w n", w=QUARTER),
                        iota_b[:, :].unsqueeze(1).unsqueeze(1).to_broadcast([P, WIN_TILES, QUARTER, P]),
                        cols[:, 1, :, c * QUARTER:(c + 1) * QUARTER].unsqueeze(3)
                        .to_broadcast([P, WIN_TILES, QUARTER, P]), ALU.is_equal).then_inc(build_hot, 1)
                chain.leave(TILES)
            dve.wait_ge(cells_copied, 4 * TILES + 2)
            dve.wait_ge(block_stored, 16 * TILES)
            chain(dve.tensor_reduce(bad[:, 1:2], over[:, :], AX.X, ALU.max))
            dve.tensor_tensor(bad[:, 0:1], bad[:, 0:1], bad[:, 1:2], ALU.max).then_inc(bad_ready, 1)
            dve.wait_ge(bad_summed, 1)
            dve.tensor_scalar(ok_i[:, :], ps_bad, 0.0, None, ALU.is_equal).then_inc(ok_ready, 1)
            dve.wait_ge(ok_ready, 1)
            dense = dve.value_load(ok_i[0:1, 0:1], min_val=0, max_val=1)
            end_stage(dve.tensor_copy(col[:, 7:8], col[:, 7:8]), 0)

            masks = [keep[:, :], crossT[:, :], join]

            def dense_pass(n, source, scale):
                step = dense_chain
                step(dve.tensor_copy(parts[:, :, 0, :], source[:, :, :]))
                step(dve.tensor_tensor(tmp[:, :, :], source[:, :, :], parts[:, :, 0, :], ALU.subtract))
                step(dve.tensor_copy(parts[:, :, 1, :], tmp[:, :, :]))
                dve.tensor_tensor(parts[:, :, 2, :], tmp[:, :, :], parts[:, :, 1, :], ALU.subtract
                                  ).then_inc(parts_ready, 1)
                with dve.Fori(0, GROUPS) as r:
                    step.enter(r, GROUP)
                    for b in range(GROUP):
                        buf = b % A_BUFS
                        uses = len(range(buf, GROUP, A_BUFS))
                        dve.wait_ge(a_used[buf], r * uses + uses * GROUPS * n + b // A_BUFS + 2)
                        dve.wait_ge(acc_used, r * GROUP + TILES * n + b + GROUP)
                        step(dve.tensor_reduce(part_sum[:, b % 2, :],
                                               ps[:, b, 0:PARTS * D].rearrange("p (k f) -> p f k", k=PARTS),
                                               AX.X, ALU.add))
                        dve.tensor_scalar(agg[:, bass.ds(r * GROUP + b, 1), :].rearrange("p t f -> p (t f)"),
                                          part_sum[:, b % 2, :], scale[:, bass.ds(r * GROUP + b, 1)], None, ALU.mult
                                          ).then_inc(acc_used, 1)
                    step.leave(GROUPS)
                dve.wait_ge(acc_used, TILES * (n + 1) + GROUP)

            def edge_pass(how, n, scale):
                q, step = sets[how], gather_chain[how]
                op0, op1 = (ALU.mult, ALU.add) if how == "sum" else (ALU.min, ALU.max)
                step(dve.memset(run[:, 1, HALF - 1, :], 0.0))
                for hf in range(2):
                    dve.tensor_copy(idx_stage[:, hf, :], src[:, hf * HALF:(hf + 1) * HALF]
                                    ).then_inc(q["idx_ready"][hf], 1)
                with dve.Fori(0, STEPS) as r:
                    step.enter(r, 2 * HALF)
                    for hf in range(2):
                        step(dve.tensor_copy(keep_stage[:, hf, :], keep[:, bass.ds(r * STEP + hf * HALF, HALF)]))
                        dve.wait_ge(q["gathered"][n][hf], r * (16 * HALF) + 16 * HALF)
                        dve.tensor_copy(idx_stage[:, hf, :], src[:, bass.ds(r * STEP + STEP + hf * HALF, HALF)]
                                        ).then_inc(q["idx_ready"][hf], 1)
                        if how == "max":
                            dve.wait_ge(edge_ready[hf], r + STEPS * n + 2)
                            v = msg[:, hf, :, :].rearrange("p (g q) f -> p g (q f)", q=QUAD)
                            dve.tensor_tensor(v, v, ps_edge, ALU.add).then_inc(edge_used, 1)
                            dve.wait_ge(edge_used, r * 2 + 2 * STEPS * n + hf + 2)
                        dve.wait_ge(q["stored"][hf], r * 16 + 16 * STEPS * n + 16)
                        prev = run[:, 1 - hf, HALF - 1, :]
                        for s in range(HALF):
                            last = dve.scalar_tensor_tensor(
                                out=run[:, hf, s, :], in0=prev, scalar=keep_stage[:, hf, s:s + 1],
                                in1=msg[:, hf, s, :], op0=op0, op1=op1)
                            prev = run[:, hf, s, :]
                            if s < HALF - 1:
                                step(last)
                        last.then_inc(q["scanned"][hf], 1)
                        dve.wait_ge(q["scanned"][hf], r + STEPS * n + 2)
                    step.leave(STEPS)
                dve.wait_ge(q["lastT_ready"], n + 1)
                dve.tensor_tensor_scan(chainT[:, 1:P + 1], crossT[:, :], ps_lastT, 0.0, op0, op1
                                       ).then_inc(q["chain_ready"], 1)
                dve.wait_ge(q["carry_ready"], n + 1)
                dve.wait_ge(q["row_gathered"], 16 * (n + 1))
                dve.scalar_tensor_tensor(out=fixed[:, :], in0=ps_carry, scalar=join, in1=fix_row[:, :],
                                         op0=op0, op1=op1).then_inc(q["row_fixed"], 1)
                dve.wait_ge(q["agg_gathered"], 16 * TILES * (n + 1))
                step(dve.tensor_tensor(agg[:, :, :], agg[:, :, :], over_features(scale[:, :]), ALU.mult))

            roots = sums = groups = 0
            for i, k, stage in numbered():
                if stage[0] == "norm":
                    roots += 1
                    m, v = stat[:, 0, :], stat[:, 1, :]
                    chain(dve.tensor_reduce(m, x[:, :, :], AX.X, ALU.add))
                    chain(dve.tensor_scalar(m, m, -1.0 / D, None, ALU.mult))
                    chain(dve.tensor_tensor(tmp[:, :, :], x[:, :, :], over_features(m), ALU.add))
                    chain(dve.tensor_tensor(h[:, :, :], tmp[:, :, :], tmp[:, :, :], ALU.mult))
                    chain(dve.tensor_reduce(v, h[:, :, :], AX.X, ALU.add))
                    dve.tensor_scalar(v, v, 1.0 / D, EPS, ALU.mult, ALU.add).then_inc(std_in, 1)
                    dve.wait_ge(std_out, roots)
                    chain(dve.reciprocal(v, v))
                    chain(dve.tensor_tensor(h[:, :, :], tmp[:, :, :], over_features(v), ALU.mult))
                    end_stage(dve.tensor_scalar(h[:, :, :], h[:, :, :], 0.0, None, ALU.max), i)

                elif stage[0] == "project":
                    _, _, how, to = stage
                    to = node_tile[to]
                    steps = {"relu": 0, "add": 0, "copy": 0, "leaky": 1, "leaky_add": 2}[how]
                    with dve.Fori(0, GROUPS) as r:
                        chain.enter(r, steps)
                        at = (slice(None), bass.ds(r * GROUP, GROUP), slice(None))
                        dve.wait_ge(projected, r + GROUPS * k + 2)
                        if how == "relu":
                            last = dve.tensor_scalar(to[at], ps_out, 0.0, None, ALU.max)
                        elif how == "add":
                            last = dve.tensor_tensor(to[at], to[at], ps_out, ALU.add)
                        elif how == "copy":
                            last = dve.tensor_copy(to[at], ps_out)
                        else:
                            chain(dve.tensor_tensor(tmp[at], agg[at], ps_out, ALU.add))
                            c = h2 if how == "leaky" else tmp
                            last = dve.scalar_tensor_tensor(out=c[at], in0=tmp[at], scalar=0.01, in1=tmp[at],
                                                            op0=ALU.mult, op1=ALU.max)
                            if how == "leaky_add":
                                chain(last)
                                last = dve.tensor_tensor(x[at], x[at], tmp[at], ALU.add)
                        last.then_inc(drained, 1)
                        chain.leave(GROUPS)
                    dve.wait_ge(drained, GROUPS * (k + 1) + 1)
                    end_stage(dve.tensor_copy(col[:, 7:8], col[:, 7:8]), i)

                elif stage[0] == "graphnorm":
                    _, which, identity, to = stage
                    w, b, scale = (norm_p[:, 3 * which + j, :] for j in range(3))

                    def mask_pads():
                        chain(dve.tensor_scalar(tmp[:, LAST, :], tmp[:, LAST, :], valid, None, ALU.mult))

                    def sum_nodes(v):
                        dve.tensor_reduce(g_sum[:, :], v[:, :, :].rearrange("p t f -> p f t"), AX.X,
                                          ALU.add).then_inc(sum_in, 1)

                    mask_pads()
                    sum_nodes(tmp)
                    sums += 1
                    dve.wait_ge(sum_out, sums)
                    chain(dve.tensor_scalar(g_a[:, :], ps_stat, -1.0 / N, None, ALU.mult))
                    chain(dve.tensor_tensor(g_a[:, :], g_a[:, :], scale, ALU.mult))
                    chain(dve.tensor_tensor(tmp[:, :, :], tmp[:, :, :], over_tiles(g_a[:, :]), ALU.add))
                    mask_pads()
                    chain(dve.tensor_tensor(agg[:, :, :], tmp[:, :, :], tmp[:, :, :], ALU.mult))
                    sum_nodes(agg)
                    sums += 1
                    dve.wait_ge(sum_out, sums)
                    roots += 1
                    dve.tensor_scalar(g_b[:, :], ps_stat, 1.0 / N, EPS, ALU.mult, ALU.add).then_inc(std_in, 1)
                    dve.wait_ge(std_out, roots)
                    chain(dve.reciprocal(g_b[:, :], g_b[:, :]))
                    chain(dve.tensor_tensor(g_b[:, :], g_b[:, :], w, ALU.mult))
                    chain(dve.tensor_tensor(tmp[:, :, :], tmp[:, :, :], over_tiles(g_b[:, :]), ALU.mult))
                    chain(dve.tensor_tensor(tmp[:, :, :], tmp[:, :, :], over_tiles(b), ALU.add))
                    last = dve.scalar_tensor_tensor(
                        out=h2[:, :, :], in0=tmp[:, :, :], scalar=0.0,
                        in1=node_tile[identity][:, :, :], op0=ALU.max, op1=ALU.add)
                    if to == "x":
                        chain(last)
                        last = dve.tensor_tensor(x[:, :, :], x[:, :, :], h2[:, :, :], ALU.add)
                    end_stage(last, i)

                elif stage[0] == "edges":
                    how, n = place(k)
                    scale = {"mean": mean_scale, "some": some}[stage[3]]
                    if how == "sum":
                        with dve.If(dense):
                            dense_pass(n, node_tile[stage[1]], scale)
                        with dve.Else():
                            edge_pass(how, n, scale)
                    else:
                        if n == 0:
                            for v in masks:
                                chain(dve.tensor_scalar(v, v, 2.0, -1.0, ALU.mult, ALU.add))
                                chain(dve.tensor_scalar(v, v, BIG, None, ALU.mult))
                        edge_pass(how, n, scale)
                        if n == 1:
                            for v in masks:
                                chain(dve.tensor_scalar(v, v, 0.0, None, ALU.is_gt))
                    end_stage(dve.tensor_copy(col[:, 7:8], col[:, 7:8]), i)


_INS = ["x", "src", "dst", "edge_attr_32", "L2_gnn_W1_edge", "L2_gnn_W2_edge"] + WEIGHTS + list(BIASES.values()) + NORMS


def kernel(**inputs):
    import numpy as np
    import concourse.bacc as bacc
    from concourse.bass_utils import run_bass_kernel_spmd

    nc = bacc.Bacc("TRN2", target_bir_lowering=False, num_devices=1)
    arrays, aps = {}, {}
    for name in _INS:
        v = np.ascontiguousarray(inputs[name])
        arrays[f"in_{name}"] = v
        aps[name] = nc.dram_tensor(f"in_{name}", v.shape, mybir.dt.from_np(v.dtype), kind="ExternalInput").ap()
    out = nc.dram_tensor("out", (N, D), mybir.dt.float32, kind="ExternalOutput").ap()
    build(nc, aps, out)
    r = run_bass_kernel_spmd(nc, [arrays], core_ids=[0])
    return r.results[0]["out"]
```

```python
from contextlib import ExitStack

import concourse.bass as bass
from concourse import mybir

P = 128
N, E, D, DE = 6250, 200000, 96, 32
TILES = -(-N // P)
NPAD = TILES * P
GROUP = 7
GROUPS = TILES // GROUP
HALF = 16
STEP = 2 * HALF
STEPS = -(-E // (P * STEP))
SLOTS = STEPS * STEP
TAIL = E - (P - 1) * SLOTS
MAIN, REST = 112, 15
QUAD = P // DE
PICK = 8
PICKS = SLOTS // PICK
HALF_PICKS = HALF // PICK
PICKED = [[7, 15], [7]]
PICK_HALVES = [2, 1]
SPLIT = 32
BIG = 3.4028235e38
PAD_NODE = 8191
SRC_BITS = 13
WIN = 8
WINDOWS = NPAD // WIN
ROW = 32
ROWS = P * SLOTS // ROW
WIN_TILES = 3
WIN_ROWS = WIN_TILES * P // ROW
WIN_GROUP = 112
WIN_GROUPS = WINDOWS // WIN_GROUP
WIN_BLOCKS = TILES // WIN_GROUPS
QUARTER = 4
HOT_ROWS = QUARTER * WIN_TILES
CELLS = WIN * TILES
MAX_COUNT = 16.0
A_BUFS = 4
PARTS = 3
EPS = 1e-5

WEIGHTS = ["L0_gnn_W1_l", "L0_gnn_W1_r", "L0_gnn_W2_l", "L0_gnn_W2_r", "L1_gnn_W_self",
           "L1_gnn_W_neigh", "L2_gnn_W1_msg", "L2_gnn_W1_root", "L2_gnn_W2_msg",
           "L2_gnn_W2_root", "L3_gnn_W1", "L3_gnn_W2"]
BIASES = {"L0_gnn_W1_l": "L0_gnn_b1", "L0_gnn_W2_l": "L0_gnn_b2", "L1_gnn_W_self": "L1_gnn_b",
          "L2_gnn_W1_root": "L2_gnn_b1", "L2_gnn_W2_root": "L2_gnn_b2",
          "L3_gnn_W1": "L3_gnn_b1", "L3_gnn_W2": "L3_gnn_b2"}
NORMS = ["L3_gnn_gn1_w", "L3_gnn_gn1_b", "L3_gnn_gn1_a", "L3_gnn_gn2_w", "L3_gnn_gn2_b",
         "L3_gnn_gn2_a"]

STAGES = [
    ("setup",),
    ("norm", "norm parts"),
    ("edges", "h", "sum", "mean", None),
    ("project", [("agg", "L0_gnn_W1_l"), ("h", "L0_gnn_W1_r")], "relu", "h2", "parts", None),
    ("edges", "h2", "sum", "mean", None),
    ("project", [("agg", "L0_gnn_W2_l"), ("h2", "L0_gnn_W2_r")], "add", "x", "norm parts", None),
    ("edges", "h", "sum", "mean", None),
    ("project", [("h", "L1_gnn_W_self"), ("agg", "L1_gnn_W_neigh")], "add", "x", "norm", None),
    ("project", [("h", "L2_gnn_W1_msg")], "copy", "agg", "", None),
    ("edges", "agg", "max", "some", ("h", "L2_gnn_W1_root", "h2")),
    ("project", [("h2", "L2_gnn_W2_msg")], "copy", "agg", "", (0, "h2", "leaky")),
    ("edges", "agg", "max", "some", ("h2", "L2_gnn_W2_root", "h")),
    ("combine", (1, "h", "leaky_add"), "norm parts"),
    ("edges", "h", "sum", "some", None),
    ("project", [("agg", "L3_gnn_W1")], "copy", "agg2", "", None),
    ("graphnorm", 0, "h", "h2"),
    ("edges", "h2", "sum", "some", None),
    ("project", [("agg", "L3_gnn_W2")], "copy", "agg2", "", None),
    ("graphnorm", 1, "h2", "x"),
]


def numbered():
    seen = {}
    for i, s in enumerate(STAGES):
        yield i, seen.get(s[0], 0), s
        seen[s[0]] = seen.get(s[0], 0) + 1


PASSES = [s for s in STAGES if s[0] == "edges"]
LOADS = 2 + len(WEIGHTS) + len(BIASES) + 2 * QUAD + len(NORMS)


class Chain:

    def __init__(self, engine, sem):
        self.engine, self.sem, self.n, self.reg, self.per = engine, sem, 0, None, 0

    def __call__(self, ins):
        self.n += 1
        ins.then_inc(self.sem, 1)
        self.engine.wait_ge(self.sem, self.n if self.reg is None else self.reg * self.per + self.n)

    def enter(self, reg, per, first=0):
        self.reg, self.per, self.at, self.first = reg, per, self.n, first
        self.n -= first * per

    def leave(self, trips):
        assert self.n == self.at + self.per - self.first * self.per
        self.n, self.reg = self.at + self.per * trips, None


def place(k):
    how = PASSES[k][2]
    return how, sum(s[2] == how for s in PASSES[:k])


def build(nc, a, out):
    f32, bf16, i32, f8 = mybir.dt.float32, mybir.dt.bfloat16, mybir.dt.int32, mybir.dt.float8e4
    ALU = mybir.AluOpType
    ACT = mybir.ActivationFunctionType
    AX = mybir.AxisListType

    with ExitStack() as ctx:
        def sb(name, shape, dt=f32):
            return ctx.enter_context(nc.sbuf_tensor(name, shape, dt))

        def sem(name):
            return ctx.enter_context(nc.semaphore(name))

        table = nc.dram_tensor("table", (NPAD, D), f32, kind="Internal").ap()
        running = nc.dram_tensor("running", (P * SLOTS, D), f32, kind="Internal").ap()
        keys = nc.dram_tensor("keys", (ROWS, ROW), i32, kind="Internal").ap()
        sample_rows = nc.dram_tensor("sample_rows", (P, SLOTS // ROW), f32, kind="Internal").ap()
        picked = nc.dram_tensor("picked", (PICKS, P), mybir.dt.int16, kind="Internal").ap()
        starts = nc.dram_tensor("starts", (NPAD + 1,), f32, kind="Internal").ap()
        adjacency = nc.dram_tensor("adjacency", (TILES, P, TILES * P // 2), bf16, kind="Internal").ap()
        edge_tail = nc.dram_tensor("edge_tail", (SLOTS, DE), f32, kind="Internal").ap()

        x = sb("x_sb", [P, TILES, D])
        h = sb("h_sb", [P, TILES, D])
        h2 = sb("h2_sb", [P, TILES, D])
        agg = sb("agg_sb", [P, TILES, D])
        tmp = sb("tmp_sb", [P, TILES, D])
        node_tile = {"x": x, "h": h, "h2": h2, "agg": agg, "agg2": tmp}
        src = sb("src_sb", [P, SLOTS + STEP], i32)
        dst_f = sb("dst_f", [P, SLOTS])
        keep = sb("keep", [P, SLOTS])
        idx_stage = sb("idx_stage", [P, 2, HALF], i32)
        keep_stage = sb("keep_stage", [P, 2, HALF])
        RUN_WORDS = 2 * HALF * D
        EDGE_WORDS, BLOCK_WORDS = 2 * RUN_WORDS + 2 * HALF * DE, TILES * P // 4
        edge_and_blocks = sb("edge_and_blocks", [P, EDGE_WORDS + A_BUFS * BLOCK_WORDS])
        edge_buf = edge_and_blocks[:, 0:EDGE_WORDS]
        msg = edge_buf[:, 0:RUN_WORDS].rearrange("p (b s f) -> p b s f", b=2, f=D)
        run = edge_buf[:, RUN_WORDS:2 * RUN_WORDS].rearrange("p (b s f) -> p b s f", b=2, f=D)
        ea = edge_buf[:, 2 * RUN_WORDS:].rearrange("p (b s f) -> p b s f", b=2, f=DE)
        parts = edge_buf[:, 0:TILES * PARTS * D // 2].bitcast(bf16).rearrange("p (t k f) -> p t k f", k=PARTS, f=D)
        a_buf = edge_and_blocks[:, EDGE_WORDS:].bitcast(f8).rearrange("p (a t n) -> p a t n", t=TILES, n=P)
        block_stage = (edge_and_blocks[:, EDGE_WORDS + (A_BUFS - WIN_BLOCKS) * BLOCK_WORDS:].bitcast(f8)
                       .rearrange("p (a t n) -> p a t n", t=TILES, n=P))
        hot = (edge_and_blocks[:, EDGE_WORDS:].bitcast(bf16)
               .rearrange("p (i t n) -> p i t n", i=HALF_PICKS, n=P))
        pick_row = sb("pick_row", [P, 2, HALF_PICKS * P], mybir.dt.int16)
        node_code = sb("node_code", [P, TILES, 2], mybir.dt.int16)
        part_sum = sb("part_sum", [P, 2, D])
        eaT = sb("eaT", [P, 2, HALF // QUAD, P])
        fix_row = sb("fix_row", [P, D])
        fixed = sb("fixed", [P, D])
        chainT = sb("chainT", [D, P + 1])
        ident = sb("ident", [P, P])
        ones = sb("ones", [P, P])
        over = sb("over", [P, 4 * TILES])
        neg_max = sb("neg_max", [P, 1])
        bad = sb("bad", [P, 2])
        ok_i = sb("ok_i", [P, 1], i32)
        win_i = sb("win_i", [WIN_GROUP, WIN_GROUPS], i32)
        v_w = sb("v_w", [WIN_GROUP, WIN_GROUPS])
        v_n = sb("v_n", [P, TILES])
        node_i = sb("node_i", [P, TILES], i32)
        samples = sb("samples", [P, TILES])
        firsts = sb("firsts", [P, P])
        find_w = [sb(f"find_w{i}", [WIN_GROUP, WIN_GROUPS]) for i in range(2)]
        find_n = [sb(f"find_n{i}", [P, TILES]) for i in range(2)]
        idx_w = sb("idx_w", [WIN_GROUP, WIN_GROUPS], i32)
        idx_n = sb("idx_n", [P, TILES], i32)
        need_w = sb("need_w", [WIN_GROUP, WIN_GROUPS])
        base_w = sb("base_w", [WIN_GROUP, WIN_GROUPS])
        ramp = sb("ramp", [WIN_GROUP, WIN_GROUPS, WIN_ROWS], i32)
        ramp_f = sb("ramp_f", [WIN_GROUP, WIN_GROUPS, WIN_ROWS])
        rows_w = sb("rows_w", [WIN_GROUP, WIN_GROUPS, WIN_ROWS], i32)
        cols = sb("cols", [P, 2, HOT_ROWS * P // (WIN * QUARTER), 2], mybir.dt.int16)
        start_n = sb("start_n", [P, TILES])
        iota_c = sb("iota_c", [P, CELLS], mybir.dt.int16)

        def inside(tile, at, shape, dt):
            n = 1
            for v in shape[1:]:
                n *= v
            size = {f32: 4, i32: 4, bf16: 2, mybir.dt.int16: 2, f8: 1}[dt]
            assert at * 4 + n * size <= TILES * D * 4 and n * size % 4 == 0
            v = tile[:, :, :].rearrange("p t f -> p (t f)")[0:shape[0], at:at + n * size // 4]
            v = v if dt == f32 else v.bitcast(dt)
            names = "abcd"[:len(shape) - 1]
            if len(names) == 1:
                return v
            return v.rearrange(f"p ({' '.join(names)}) -> p {' '.join(names)}",
                               **{c: m for c, m in zip(names, shape[1:])})

        part_i = inside(agg, 0, [P, SLOTS], i32)
        key_i = inside(h2, 0, [P, SLOTS], i32)
        near_w = inside(agg, SLOTS, [WIN_GROUP, WIN_GROUPS, P], f32)
        samples_w = inside(agg, SLOTS + WIN_GROUPS * P, [WIN_GROUP, WIN_GROUPS, SLOTS // ROW], f32)
        keys_w = inside(agg, 2 * SLOTS, [WIN_GROUP, WIN_GROUPS, ROW], i32)
        near_n = inside(tmp, SLOTS, [P, TILES, P], bf16)
        samples_n = inside(x, 0, [P, TILES, SLOTS // ROW], f32)
        keys_n = inside(x, TILES * TILES, [P, TILES, ROW], i32)
        AFTER = TILES * (TILES + ROW)
        picked_f = inside(x, AFTER, [P, 2, PICKS // 2], f32)
        picked_i = inside(x, AFTER + PICKS, [PICKS // 2, 2, P], mybir.dt.int16)
        pick_parts = [inside(tmp, 0, [P, SPLIT, PARTS, D], bf16), inside(agg, 0, [P, TILES - SPLIT, PARTS, D], bf16)]
        win_keys = inside(h, SLOTS, [WIN_GROUP, 2, WIN_TILES * P], i32)
        win_tmp = inside(h, SLOTS + 2 * WIN_TILES * P, [WIN_GROUP, 2, WIN_TILES * P], i32)
        decoded = inside(h, SLOTS + 4 * WIN_TILES * P, [WIN_GROUP, 2, 2, WIN_TILES * P], f32)
        colsT = inside(h2, 0, [P, 2, WINDOWS // QUARTER, WIN_TILES, QUARTER], f32)
        cell_hot = inside(tmp, 0, [P, 2, HOT_ROWS, CELLS], bf16)
        low_hot = inside(agg, 0, [P, 2, HOT_ROWS, P], bf16)
        junk = inside(agg, HOT_ROWS * P, [P, 2, QUARTER * CELLS], f32)
        count = sb("count", [P, TILES])
        end_i = sb("end_i", [P, TILES], i32)
        some = sb("some", [P, TILES])
        mean_scale = sb("mean_scale", [P, TILES])
        group_mean = sb("group_mean", [P, GROUP])
        group_var = sb("group_var", [P, GROUP])
        prev_i = sb("prev_i", [P, 1], i32)
        col = sb("col", [P, 8])
        first_i = sb("first_i", [P, 1], i32)
        start_i = sb("start_i", [P, 1], i32)
        wide = sb("wide", [P, D])
        crossT = sb("crossT", [D, P])
        w_all = sb("w_all", [D + 1, len(WEIGHTS), D])
        w_edge = sb("w_edge", [P, 2, QUAD, D])
        norm_p = sb("norm_p", [P, len(NORMS), D])
        node_stage = sb("node_stage", [P, 2, GROUP, D])
        nodeT = sb("nodeT", [D + 1, 2, GROUP, P])
        g_sum = sb("g_sum", [P, D])
        g_a = sb("g_a", [P, D])
        g_b = sb("g_b", [P, D])
        ps = ctx.enter_context(nc.psum_tensor("ps", [P, 8, 512], f32))

        ps_nodeT = [ps[0:D, 2 * i:2 * i + 2, :].rearrange("p b (t n) -> p (b t) n", n=P)[:, 0:GROUP, :]
                    for i in range(2)]
        ps_out = ps[:, 4:6, :].rearrange("p b (t n) -> p (b t) n", n=P)[:, 0:GROUP, 0:D]
        ps_eaT = ps[:, 0, :].rearrange("p (q n) -> p q n", n=P)
        ps_pick = [ps[:, 1, 0:PARTS * D], ps[:, 6, 0:PARTS * D]]
        ps_pickedT = ps[0:PICKS // 2, 5, 0:2 * P].rearrange("p (v n) -> p v n", n=P)
        ps_edge = ps[:, 2:6, 0:QUAD * D]
        ps_dec = ps[:, 0:2 * WIN_TILES, CELLS:CELLS + WIN_GROUP].rearrange("p (v k) n -> p v k n", v=2)
        ps_cells = ps[:, :, 0:CELLS].rearrange("p (b w) c -> p b w c", b=2)
        ps_rootT = ps[0:D, 7, 0:P]
        ps_root = ps[:, 7, 384:384 + D]
        ps_bad = ps[:, 7, 0:1]
        ps_firsts = ps[:, 6, 0:P]
        ps_lastT = ps[0:D, 7, 0:P]
        ps_carry = ps[:, 7, 128:128 + D]
        ps_stat = ps[:, 7, 256:256 + D]

        stage_done = sem("stage_done")
        dve_done = sem("dve_done")
        loaded = sem("loaded")
        src_loaded = sem("src_loaded")
        x_loaded = sem("x_loaded")
        nodes_found = sem("nodes_found")
        dst_loaded = sem("dst_loaded")
        zeroed = sem("zeroed")
        ready = sem("constants_ready")
        pool_made = sem("pool_made")
        wide_ready = sem("wide_ready")
        wideT_ready = sem("wideT_ready")
        crossT_copied = sem("crossT_copied")
        staged = sem("staged")
        transposed = sem("transposed")
        lhs_ready = sem("lhs_ready")
        projected = sem("projected")
        drained = sem("drained")
        std_in = sem("std_in")
        std_out = sem("std_out")
        sum_in = sem("sum_in")
        sum_out = sem("sum_out")
        def edge_set(name, passes):
            return dict(
                steps=sem(f"{name}_steps"),
                table_stored=sem(f"{name}_table_stored"),
                idx_ready=[sem(f"{name}_idx_ready{i}") for i in range(2)],
                gathered=[[sem(f"{name}_gathered{n}_{i}") for i in range(2)] for n in range(passes)],
                scanned=[sem(f"{name}_scanned{i}") for i in range(2)],
                stored=[sem(f"{name}_stored{i}") for i in range(2)],
                lastT_ready=sem(f"{name}_lastT_ready"),
                chain_ready=sem(f"{name}_chain_ready"),
                carry_ready=sem(f"{name}_carry_ready"),
                row_gathered=sem(f"{name}_row_gathered"),
                row_fixed=sem(f"{name}_row_fixed"),
                row_stored=sem(f"{name}_row_stored"),
                agg_gathered=[sem(f"{name}_agg_gathered{g}") for g in range(GROUPS)])

        sets = {"sum": edge_set("sum", 5), "max": edge_set("max", 2)}
        ea_loaded = [sem(f"ea_loaded{i}") for i in range(2)]
        ea_turned = [sem(f"ea_turned{i}") for i in range(2)]
        eaT_ready = [sem(f"eaT_ready{i}") for i in range(2)]
        edge_ready = [sem(f"edge_ready{i}") for i in range(2)]
        edge_used = sem("edge_used")
        picked_stored = sem("picked_stored")
        pick_loaded = [sem(f"pick_loaded{i}") for i in range(2)]
        hot_ready = [sem(f"hot_ready{i}") for i in range(HALF_PICKS)]
        pick_ready = [sem(f"pick_ready{i}") for i in range(HALF_PICKS)]
        pick_read = [sem(f"pick_read{i}") for i in range(HALF_PICKS)]
        root_staged = sem("root_staged")
        root_turned = sem("root_turned")
        root_lhs_ready = sem("root_lhs_ready")
        root_projected = sem("root_projected")
        root_copied = sem("root_copied")
        combined = sem("combined")
        keys_made = sem("keys_made")
        keys_stored = sem("keys_stored")
        firsts_wide = sem("firsts_wide")
        firsts_turned = sem("firsts_turned")
        find_ready = sem("find_ready")
        found = [sem(f"found{i}") for i in range(4)]
        starts_made = sem("starts_made")
        starts_stored = sem("starts_stored")
        starts_loaded = sem("starts_loaded")
        rows_ready = sem("rows_ready")
        win_gathered = [sem(f"win_gathered{i}") for i in range(2)]
        decoded_ready = sem("decoded_ready")
        dec_turned = sem("dec_turned")
        colsT_ready = sem("colsT_ready")
        build_hot = sem("build_hot")
        cells_ready = sem("cells_ready")
        cells_copied = sem("cells_copied")
        block_stored = sem("block_stored")
        stage_free = sem("stage_free")
        bad_ready = sem("bad_ready")
        bad_summed = sem("bad_summed")
        ok_ready = sem("ok_ready")
        dense_steps = sem("dense_steps")
        a_loaded = [sem(f"a_loaded{i}") for i in range(A_BUFS)]
        a_used = [sem(f"a_used{i}") for i in range(A_BUFS)]
        acc_used = sem("acc_used")
        out_stored = sem("out_stored")
        marks = sem("marks")

        EDGE_PARTS = [(0, MAIN), (MAIN, P - 1), (P - 1, P)]

        def by_tile(v):
            return v.rearrange("(t p) f -> p t f", p=P)

        running_rows = running.rearrange("(p s) f -> p (s f)", p=P)
        dst_i = tmp[:, :, :].bitcast(i32).rearrange("p t f -> p (t f)")[:, 0:SLOTS]
        scratch = h[:, :, :].rearrange("p t f -> p (t f)")[:, 0:SLOTS]
        valid, prev_f, join, full, cross, first_n, first_f, start_f = (col[:, i:i + 1] for i in range(8))
        LAST = TILES - 1
        LAST_N = N - LAST * P

        block = ctx.enter_context(nc.Block())

        @block.sync
        def _(sp):
            def load_edges(to, v, done):
                for p0, p1 in EDGE_PARTS:
                    part = v[p0 * SLOTS:min(p1 * SLOTS, E)]
                    w = part.shape[0] // (p1 - p0)
                    sp.dma_start(to[p0:p1, 0:w], part.rearrange("(p s) -> p s", s=w)).then_inc(done, 16)

            def store_running(r, hf, q, n):
                sp.wait_ge(q["scanned"][hf], r + STEPS * n + 2)
                sp.dma_start(running_rows[:, bass.ds(r * (STEP * D) + hf * HALF * D, HALF * D)],
                             run[:, hf, :, :].rearrange("p s f -> p (s f)")).then_inc(q["stored"][hf], 16)

            def load_attributes(r, hf):
                at = bass.ds(r * (STEP * DE) + hf * HALF * DE, HALF * DE)
                for p0, p1 in EDGE_PARTS:
                    v = a["edge_attr_32"][p0 * SLOTS:p1 * SLOTS, :] if p1 < P else edge_tail
                    sp.dma_start(ea[p0:p1, hf, :, :].rearrange("p s f -> p (s f)"),
                                 v.rearrange("(p s) f -> p (s f)", s=SLOTS)[:, at]).then_inc(ea_loaded[hf], 16)

            sp.sem_inc(stage_free, WIN_BLOCKS)
            sp.wait_ge(zeroed, 1)
            for i, q in enumerate(sets.values()):
                for hf in range(2):
                    sp.dma_start(running_rows[:, (2 * i + hf) * HALF * D:(2 * i + hf + 1) * HALF * D],
                                 edge_buf[:, 0:HALF * D]).then_inc(q["stored"][hf], 16)
            load_edges(dst_i, a["dst"], dst_loaded)
            with nc.allow_non_contiguous_dma(reason="one word for each partition"):
                sp.dma_start(prev_i[1:P, :], a["dst"][SLOTS - 1:(P - 1) * SLOTS:SLOTS].unsqueeze(1)
                             ).then_inc(dst_loaded, 16)
            load_edges(src, a["src"], src_loaded)
            sp.wait_ge(keys_made, 1)
            sp.dma_start(keys.rearrange("(p r) c -> p (r c)", p=P), key_i).then_inc(keys_stored, 16)
            sp.dma_start(sample_rows, samples[:, :]).then_inc(keys_stored, 16)
            sp.dma_start(edge_tail[0:TAIL, :], a["edge_attr_32"][E - TAIL:E, :]).then_inc(loaded, 16)
            sp.dma_start(edge_tail[TAIL:SLOTS, :].rearrange("(p q) f -> p (q f)", p=64),
                         edge_buf[0:64, 0:(SLOTS - TAIL) * DE // 64]
                         ).then_inc(loaded, 16)
            for i, name in enumerate(WEIGHTS):
                sp.dma_start(w_all[0:D, i, :], a[name]).then_inc(loaded, 16)
                if name in BIASES:
                    sp.dma_start(w_all[D:D + 1, i, :], a[BIASES[name]].unsqueeze(0)).then_inc(loaded, 16)
            for i, name in enumerate(("L2_gnn_W1_edge", "L2_gnn_W2_edge")):
                for q in range(QUAD):
                    sp.dma_start(w_edge[q * DE:(q + 1) * DE, i, q, :], a[name]).then_inc(loaded, 16)
            for i, name in enumerate(NORMS):
                sp.dma_start(norm_p[:, i, :], a[name].unsqueeze(0).to_broadcast([P, D])).then_inc(loaded, 16)

            sp.wait_ge(crossT_copied, 1)
            sp.dma_start(picked.rearrange("(v c) n -> c v n", v=2), picked_i).then_inc(picked_stored, 16)

            def load_picks(step, hf):
                n = HALF_PICKS * P
                sp.dma_start(pick_row[:, hf, :], picked.rearrange("c n -> (c n)")[bass.ds(step * (2 * n) + hf * n, n)]
                             .unsqueeze(0).to_broadcast([P, n])).then_inc(pick_loaded[hf], 16)

            def store_blocks(first, end):
                with sp.Fori(first, end) as g:
                    for i in range(WIN_BLOCKS):
                        sp.wait_ge(cells_copied, g * (4 * WIN_BLOCKS) + 4 * i + 4 + 2)
                        sp.sem_inc(marks, 1)
                        sp.dma_start(adjacency[bass.ds(g * WIN_BLOCKS + i, 1), :, :].rearrange("a p n -> (a p) n"),
                                     block_stage[:, i, :, :].rearrange("p t n -> p (t n)").bitcast(bf16)
                                     ).then_inc(block_stored, 16)
                        sp.wait_ge(block_stored, g * (16 * WIN_BLOCKS) + 16 * i + 16)
                        sp.sem_inc(stage_free, 1)

            store_blocks(0, 6)
            sp.wait_ge(starts_made, 1)
            with nc.allow_non_contiguous_dma(reason="single words: one for each node"):
                sp.dma_start(starts[1:NPAD + 1].rearrange("(t p) -> p t", p=P), find_n[1][:, :]
                             ).then_inc(starts_stored, 16)
                sp.dma_start(starts[0:1].unsqueeze(0), keep[0:1, 0:1]).then_inc(starts_stored, 16)
                sp.wait_ge(starts_stored, 32)
                sp.dma_start(start_n[:, :], starts[0:NPAD].rearrange("(t p) -> p t", p=P)).then_inc(starts_loaded, 16)
            store_blocks(6, WIN_GROUPS)

            sp.wait_ge(ok_ready, 1)
            dense = sp.value_load(ok_i[0:1, 0:1], min_val=0, max_val=1)
            for i, k, stage in numbered():
                if stage[0] != "edges":
                    continue
                how, n = place(k)
                q = sets[how]
                if how == "sum":
                    with sp.If(dense):
                        with sp.Fori(0, GROUPS) as r:
                            for b in range(GROUP):
                                uses = len(range(b % A_BUFS, GROUP, A_BUFS))
                                sp.wait_ge(a_used[b % A_BUFS], r * uses + uses * GROUPS * n + b // A_BUFS + 1)
                                sp.dma_start(a_buf[:, b % A_BUFS, :, :].rearrange("p t n -> p (t n)").bitcast(bf16),
                                             adjacency[bass.ds(r * GROUP + b, 1), :, :].rearrange("a p n -> (a p) n")
                                             ).then_inc(a_loaded[b % A_BUFS], 16)
                    with sp.Else():
                        sp.wait_ge(stage_done, i)
                        sp.dma_start(by_tile(table), node_tile[stage[1]][:, :, :]).then_inc(q["table_stored"], 16)
                        with sp.Fori(0, STEPS) as r:
                            for hf in range(2):
                                store_running(r, hf, q, n)
                else:
                    sp.wait_ge(stage_done, i)
                    sp.dma_start(by_tile(table), node_tile[stage[1]][:, :, :]).then_inc(q["table_stored"], 16)
                    for hf in range(2):
                        load_picks(0, hf)
                        load_attributes(0, hf)
                    with sp.Fori(0, STEPS - 1) as r:
                        for hf in range(2):
                            sp.wait_ge(hot_ready[0], r * 2 + (2 * STEPS + 1) * n + hf + 1)
                            load_picks(r + 1, hf)
                            store_running(r, hf, q, n)
                            sp.wait_ge(ea_turned[hf], r + STEPS * n + 1)
                            load_attributes(r + 1, hf)
                    sp.wait_ge(hot_ready[0], 2 * (STEPS - 1) + (2 * STEPS + 1) * n + 1)
                    load_picks(STEPS - 1, 0)
                    for hf in range(2):
                        store_running(STEPS - 1, hf, q, n)
            sp.wait_ge(stage_done, len(STAGES))
            sp.dma_start(by_tile(out[0:LAST * P, :]), x[:, 0:LAST, :]).then_inc(out_stored, 16)
            sp.dma_start(out[LAST * P:N, :], x[0:LAST_N, LAST, :]).then_inc(out_stored, 16)
            sp.wait_ge(out_stored, 32)

        @block.gpsimd
        def _(pool):
            pool.memset(ident[:, :], 0.0).then_inc(pool_made, 1)
            pool.wait_ge(pool_made, 1)
            pool.affine_select(out=ident[:, :], in_=ident[:, :], compare_op=ALU.not_equal, fill=1.0,
                               base=0, pattern=[[-1, P]], channel_multiplier=1)
            pool.iota(iota_c[:, :], pattern=[[1, CELLS]], base=0, channel_multiplier=0)
            pool.iota(node_code[:, :, :], pattern=[[P, TILES], [0, 2]], base=0, channel_multiplier=1)
            pool.iota(win_i[:, :], pattern=[[WIN_GROUP, WIN_GROUPS]], base=0, channel_multiplier=1)
            pool.iota(ramp[:, :, :], pattern=[[0, WIN_GROUPS], [1, WIN_ROWS]], base=0, channel_multiplier=0)
            pool.iota(node_i[:, :], pattern=[[P, TILES]], base=1, channel_multiplier=1)
            pool.iota(start_i[:, :], pattern=[[0, 1]], base=0, channel_multiplier=SLOTS).then_inc(ready, 1)

            def gather(to, frm, idx, done):
                pool.indirect_dma_start(to, None, frm, bass.IndirectOffsetOnAxis(ap=idx, axis=0)
                                        ).then_inc(done, 16)

            pool.wait_ge(keys_stored, 32)
            for i, (to, frm, idx) in enumerate(((samples_w, sample_rows, idx_w), (keys_w, keys, idx_w))):
                pool.wait_ge(find_ready, i + 1)
                for g in range(WIN_GROUPS):
                    gather(to[:, g, :], frm, idx[:, g:g + 1], found[i])
            pool.wait_ge(rows_ready, 1)
            for g in range(WIN_GROUPS):
                if g >= 2:
                    pool.wait_ge(decoded_ready, g - 1)
                for row in range(WIN_ROWS):
                    gather(win_keys[:, g % 2, row * ROW:(row + 1) * ROW], keys, rows_w[:, g, row:row + 1],
                           win_gathered[g % 2])

            for i, (to, frm) in enumerate(((samples_n, sample_rows), (keys_n, keys))):
                pool.wait_ge(find_ready, i + 3)
                for t in range(TILES):
                    gather(to[:, t, :], frm, idx_n[:, t:t + 1], found[i + 2])
            pool.wait_ge(nodes_found, 1)
            pool.dma_start(x[:, 0:LAST, :], by_tile(a["x"][0:LAST * P, :])).then_inc(x_loaded, 16)
            pool.dma_start(x[0:LAST_N, LAST, :], a["x"][LAST * P:N, :]).then_inc(x_loaded, 16)

            def edge_pass(q, n, slots):
                with pool.Fori(0, STEPS) as r:
                    for hf in range(2):
                        pool.wait_ge(q["table_stored"], 16 * (n + 1))
                        pool.wait_ge(q["idx_ready"][hf], r + (STEPS + 1) * n + 1)
                        pool.wait_ge(q["scanned"][hf], r + STEPS * n + 1)
                        pool.sem_inc(marks, 1)
                        for s in slots[hf]:
                            gather(msg[:, hf, s, :], table, idx_stage[:, hf, s:s + 1], q["gathered"][n][hf])
                for hf in range(2):
                    pool.wait_ge(q["stored"][hf], 16 * STEPS * (n + 1) + 16)
                gather(fix_row[:, :], running, first_i[:, :], q["row_gathered"])
                pool.wait_ge(q["row_fixed"], n + 1)
                pool.indirect_dma_start(running, bass.IndirectOffsetOnAxis(ap=first_i[:, :], axis=0),
                                        fixed[:, :], None).then_inc(q["row_stored"], 16)
                pool.wait_ge(q["row_stored"], 16 * (n + 1))
                for t in range(TILES):
                    gather(agg[:, t, :], running, end_i[:, t:t + 1], q["agg_gathered"][t // GROUP])

            pool.wait_ge(ok_ready, 1)
            dense = pool.value_load(ok_i[0:1, 0:1], min_val=0, max_val=1)
            for i, k, stage in numbered():
                if stage[0] != "edges":
                    continue
                how, n = place(k)
                if how == "max":
                    edge_pass(sets[how], n, [[s for s in range(HALF) if s not in taken] for taken in PICKED])
                else:
                    with pool.If(1 - dense):
                        edge_pass(sets[how], n, [range(HALF)] * 2)

        @block.scalar
        def _(act):
            for s in (lhs_ready, *eaT_ready):
                act.sem_inc(s, 1)
            act.sem_inc(cells_copied, 2)
            def copy_keys(g):
                act.wait_ge(dec_turned, g + 1)
                for v in range(2):
                    at = bass.ds(g * (WIN_GROUP // QUARTER), WIN_GROUP // QUARTER)
                    act.copy(colsT[:, v, at, :, :].rearrange("p q j w -> p j q w"),
                             ps_dec[:, v, :, :].rearrange("p j (q w) -> p j q w", w=QUARTER)
                             ).then_inc(colsT_ready, 1)

            def copy_blocks(g):
                for i in range(WIN_BLOCKS):
                    act.wait_ge(stage_free, g * WIN_BLOCKS + i + 1)
                    for c in range(4):
                        cells = ps_cells[:, c % 2, :, :]
                        act.wait_ge(cells_ready, g * (4 * WIN_BLOCKS) + 4 * i + c + 3)
                        act.activation(junk[:, c % 2, :].rearrange("p (w c) -> p w c", c=CELLS), cells, ACT.Relu,
                                       bias=neg_max[:, :],
                                       accum_out=over[:, bass.ds(g * (4 * WIN_BLOCKS) + 4 * i + c, 1)])
                        act.copy(block_stage[:, i, :, c * 32:(c + 1) * 32].rearrange("p t (w d) -> p w d t", d=WIN),
                                 cells.rearrange("p w (d t) -> p w d t", t=TILES), saturate=False
                                 ).then_inc(cells_copied, 1)

            copy_keys(0)
            with act.Fori(0, WIN_GROUPS - 1) as g:
                copy_keys(g + 1)
                copy_blocks(g)
            copy_blocks(WIN_GROUPS - 1)
            def group_root(r, before):
                act.wait_ge(std_in, r + before + 1)
                act.activation(group_var[:, :], group_var[:, :], ACT.Sqrt).then_inc(std_out, 1)

            roots = 0
            for i, k, stage in numbered():
                act.wait_ge(stage_done, i)
                if stage[0] == "graphnorm":
                    act.wait_ge(std_in, roots + 1)
                    act.activation(g_b[:, :], g_b[:, :], ACT.Sqrt).then_inc(std_out, 1)
                    roots += 1
                elif stage[0] in ("norm", "combine"):
                    for r in range(GROUPS):
                        group_root(r, roots)
                    roots += GROUPS
                elif stage[0] == "project":
                    n, norm, waits = len(stage[1]), "norm" in stage[4], stage[5] is not None

                    def stage_group(r):
                        act.wait_ge(transposed, r + GROUPS * k + 1)
                        if waits:
                            act.wait_ge(combined, r + 1)
                        for j, (name, _) in enumerate(stage[1]):
                            last = act.copy(node_stage[:, j, :, :],
                                            node_tile[name][:, bass.ds(r * GROUP, GROUP), :])
                        last.then_inc(staged, 1)

                    def copy_turned(r):
                        act.wait_ge(transposed, r + GROUPS * k + 2)
                        act.wait_ge(projected, r + GROUPS * k + 1)
                        for j in range(n):
                            last = act.copy(nodeT[0:D, j, :, :], ps_nodeT[j])
                        last.then_inc(lhs_ready, 1)

                    stage_group(0)
                    with act.Fori(0, GROUPS - 1) as r:
                        copy_turned(r)
                        stage_group(r + 1)
                        if norm:
                            group_root(r, roots)
                    copy_turned(GROUPS - 1)
                    if norm:
                        group_root(GROUPS - 1, roots)
                        roots += GROUPS
                elif stage[0] == "edges" and stage[2] == "max":
                    m = place(k)[1]
                    source, _, to = stage[4]
                    with act.Fori(0, STEPS) as r:
                        act.copy(node_stage[:, 0, 0, :], node_tile[source][:, bass.ds(r, 1), :]
                                 .rearrange("p t f -> p (t f)")).then_inc(root_staged, 1)
                        for hf in range(2):
                            act.wait_ge(ea_turned[hf], r + STEPS * m + 1)
                            act.wait_ge(edge_ready[hf], r + STEPS * m + 1)
                            act.copy(eaT[:, hf, :, :], ps_eaT).then_inc(eaT_ready[hf], 1)
                            if hf == 0:
                                act.wait_ge(root_turned, r + STEPS * m + 1)
                                act.copy(nodeT[0:D, 0, 0, :], ps_rootT).then_inc(root_lhs_ready, 1)
                            else:
                                act.wait_ge(root_projected, r + STEPS * m + 1)
                                act.copy(node_tile[to][:, bass.ds(r, 1), :].rearrange("p t f -> p (t f)"),
                                         ps_root).then_inc(root_copied, 1)

        @block.tensor
        def _(pe):
            for s in (transposed, projected, *edge_ready, *a_used):
                pe.sem_inc(s, 1)
            pe.sem_inc(cells_ready, 2)
            pe.wait_ge(ready, 1)
            pe.wait_ge(zeroed, 1)
            pe.wait_ge(firsts_wide, 1)
            pe.transpose(ps_firsts, firsts[:, :], ident[:, :]).then_inc(firsts_turned, 1)
            pe.wait_ge(wide_ready, 1)
            pe.transpose(ps_lastT, wide[:, :], ident[:, :])
            for v in range(2):
                last = pe.transpose(ps_pickedT[:, v, :], picked_f[:, v, :], ident[:, :])
            last.then_inc(wideT_ready, 1)

            def turn_keys(g):
                pe.wait_ge(decoded_ready, g + 1)
                if g:
                    pe.wait_ge(colsT_ready, 2 * g)
                    if g >= 2:
                        pe.wait_ge(cells_copied, 4 * WIN_BLOCKS * (g - 1) + 2)
                else:
                    pe.wait_ge(crossT_copied, 1)
                for v in range(2):
                    for j in range(WIN_TILES):
                        last = pe.transpose(ps_dec[:, v, j, :], decoded[:, g % 2, v, j * P:(j + 1) * P],
                                            ident[0:WIN_GROUP, 0:WIN_GROUP])
                last.then_inc(dec_turned, 1)

            turn_keys(0)
            for g in range(WIN_GROUPS):
                if g + 1 < WIN_GROUPS:
                    turn_keys(g + 1)
                pe.wait_ge(colsT_ready, 2 * min(g + 2, WIN_GROUPS))
                with pe.Fori(g * WIN_BLOCKS, (g + 1) * WIN_BLOCKS) as r:
                    for c in range(4):
                        pe.wait_ge(build_hot, r * 4 + c + 2)
                        pe.wait_ge(cells_copied, r * 4 + c + 1)
                        for w in range(QUARTER):
                            for j in range(WIN_TILES):
                                m = j * QUARTER + w
                                last = pe.matmul(ps_cells[:, c % 2, w, :], low_hot[:, c % 2, m, :],
                                                 cell_hot[:, c % 2, m, :], start=(j == 0), stop=(j == WIN_TILES - 1))
                        last.then_inc(cells_ready, 1)
            pe.wait_ge(bad_ready, 1)
            pe.matmul(ps_bad, ones[:, :], bad[:, 0:1], start=True, stop=True).then_inc(bad_summed, 1)
            pe.wait_ge(ok_ready, 1)
            dense = pe.value_load(ok_i[0:1, 0:1], min_val=0, max_val=1)

            def dense_pass(n):
                with pe.Fori(0, GROUPS) as r:
                    for b in range(GROUP):
                        buf = b % A_BUFS
                        uses = len(range(buf, GROUP, A_BUFS))
                        pe.wait_ge(a_loaded[buf], r * (16 * uses) + 16 * (uses * GROUPS * n + b // A_BUFS + 1))
                        pe.wait_ge(acc_used, r * GROUP + TILES * n + b + 1)
                        pe.sem_inc(marks, 1)
                        for t in range(TILES):
                            last = pe.matmul(ps[:, b, 0:PARTS * D], a_buf[:, buf, t, :],
                                             parts[:, t, :, :].rearrange("p k f -> p (k f)"),
                                             start=(t == 0), stop=(t == TILES - 1))
                        last.then_inc(a_used[buf], 1)

            def mend(q, n):
                pe.wait_ge(q["scanned"][1], STEPS * (n + 1) + 1)
                pe.transpose(ps_lastT, run[:, 1, HALF - 1, :], ident[:, :]).then_inc(q["lastT_ready"], 1)
                pe.wait_ge(q["chain_ready"], n + 1)
                pe.transpose(ps_carry, chainT[:, 0:P], ident[0:D, 0:D]).then_inc(q["carry_ready"], 1)

            sums = 0
            for i, k, stage in numbered():
                pe.wait_ge(stage_done, i)
                if stage[0] == "graphnorm":
                    for _ in range(2):
                        sums += 1
                        pe.wait_ge(sum_in, sums)
                        pe.matmul(ps_stat, ones[:, :], g_sum[:, :], start=True, stop=True).then_inc(sum_out, 1)
                elif stage[0] == "project":
                    n = len(stage[1])
                    with pe.Fori(0, GROUPS) as r:
                        pe.wait_ge(staged, r + GROUPS * k + 1)
                        pe.wait_ge(lhs_ready, r + GROUPS * k + 1)
                        for j in range(n):
                            for t in range(GROUP):
                                last = pe.transpose(ps_nodeT[j][:, t, :], node_stage[:, j, t, :], ident[:, :])
                        last.then_inc(transposed, 1)
                        pe.wait_ge(lhs_ready, r + GROUPS * k + 2)
                        pe.wait_ge(drained, r + GROUPS * k + 1)
                        for t in range(GROUP):
                            for j, (_, w) in enumerate(stage[1]):
                                last = pe.matmul(ps_out[:, t, :], nodeT[:, j, t, :], w_all[:, WEIGHTS.index(w), :],
                                                 start=(j == 0), stop=(j == n - 1))
                        last.then_inc(projected, 1)
                elif stage[0] == "edges":
                    how, m = place(k)
                    if how == "sum":
                        with pe.If(dense):
                            dense_pass(m)
                        with pe.Else():
                            mend(sets[how], m)
                    else:
                        with pe.Fori(0, STEPS) as r:
                            for hf in range(2):
                                pe.wait_ge(ea_loaded[hf], r * 48 + 48 * (STEPS * m + 1))
                                pe.wait_ge(eaT_ready[hf], r + STEPS * m + 1)
                                for g in range(HALF // QUAD):
                                    last = pe.transpose(ps_eaT[:, g, :],
                                                        ea[:, hf, g * QUAD:(g + 1) * QUAD, :].rearrange("p s f -> p (s f)"),
                                                        ident[:, :])
                                last.then_inc(ea_turned[hf], 1)
                                for p in range(len(PICKED[hf])):
                                    uses = PICK_HALVES[p]
                                    pe.wait_ge(hot_ready[p], r * uses + (uses * STEPS + 1) * m + hf + 1)
                                    pe.wait_ge(pick_read[p], r * uses + uses * STEPS * m + hf + 1)
                                    pe.sem_inc(marks, 1)
                                    for t in range(TILES):
                                        rows = pick_parts[t // SPLIT][:, t % SPLIT, :, :]
                                        last = pe.matmul(ps_pick[p], hot[:, p, t, :],
                                                         rows.rearrange("p k f -> p (k f)"),
                                                         start=(t == 0), stop=(t == TILES - 1))
                                    last.then_inc(pick_ready[p], 1)
                                pe.wait_ge(eaT_ready[hf], r + STEPS * m + 2)
                                pe.wait_ge(edge_used, r * 2 + 2 * STEPS * m + hf + 1)
                                for g in range(HALF // QUAD):
                                    last = pe.matmul(ps_edge[:, g, :], eaT[:, hf, g, :],
                                                     w_edge[:, m, :, :].rearrange("p q f -> p (q f)"),
                                                     start=True, stop=True)
                                last.then_inc(edge_ready[hf], 1)
                                if hf == 0:
                                    pe.wait_ge(root_staged, r + STEPS * m + 1)
                                    pe.transpose(ps_rootT, node_stage[:, 0, 0, :], ident[:, :]
                                                 ).then_inc(root_turned, 1)
                                else:
                                    pe.wait_ge(root_lhs_ready, r + STEPS * m + 1)
                                    pe.matmul(ps_root, nodeT[:, 0, 0, :], w_all[:, WEIGHTS.index(stage[4][1]), :],
                                              start=True, stop=True).then_inc(root_projected, 1)
                        pe.wait_ge(root_copied, STEPS * (m + 1))
                        mend(sets[how], m)

        @block.vector
        def _(dve):
            chain = Chain(dve, dve_done)
            gather_chain = {how: Chain(dve, q["steps"]) for how, q in sets.items()}
            dense_chain = Chain(dve, dense_steps)
            for s in (drained, edge_used, *pick_read, *sets["sum"]["scanned"], *sets["max"]["scanned"]):
                dve.sem_inc(s, 1)
            dve.sem_inc(acc_used, GROUP)
            dve.sem_inc(build_hot, 1)

            def end_stage(ins, i):
                ins.then_inc(stage_done, 1)
                dve.wait_ge(stage_done, i + 1)

            def over_tiles(v):
                return v.unsqueeze(1).to_broadcast([P, TILES, D])

            for v, value in ((src, 0), (dst_i, PAD_NODE), (prev_i, -1), (ones, 1.0),
                             (w_edge, 0.0), (w_all[D:D + 1, :, :], 0.0), (nodeT[D:D + 1, :, :, :], 1.0),
                             (chainT[:, 0:1], 0.0), (edge_buf, 0.0), (bad, 0.0), (neg_max, -MAX_COUNT),
                             (keep[:, 0:1], 0.0)):
                last = dve.memset(v if isinstance(v, bass.AP) else v[tuple(slice(None) for _ in v.shape)], value)
            last.then_inc(zeroed, 1)
            dve.wait_ge(zeroed, 1)
            dve.wait_ge(ready, 1)
            dve.wait_ge(dst_loaded, 64)
            chain(dve.tensor_copy(dst_f[:, :], dst_i))
            dve.tensor_copy(firsts[:, :], dst_f[:, 0:1].to_broadcast([P, P])).then_inc(firsts_wide, 1)
            dve.tensor_copy(samples[:, :], dst_f[:, 0:SLOTS:ROW])
            dve.wait_ge(src_loaded, 48)
            chain(dve.tensor_scalar(part_i, dst_i, SRC_BITS, None, ALU.logical_shift_left))
            dve.tensor_tensor(key_i, part_i, src[:, 0:SLOTS], ALU.bitwise_or).then_inc(keys_made, 1)

            def below(near, table_row, v, rows):
                shape = [near.shape[0], near.shape[1], near.shape[2]]
                chain(dve.tensor_tensor(near, table_row, v.unsqueeze(2).to_broadcast(shape), ALU.is_lt))
                chain(dve.tensor_reduce(rows, near, AX.X, ALU.add))

            def find_partition(v, near, find):
                n, g = v.shape[0], v.shape[1]
                below(near, firsts[0:n, :].unsqueeze(1).to_broadcast([n, g, P]), v, find[0][:, :])
                chain(dve.tensor_scalar(find[0][:, :], find[0][:, :], -1.0, 0.0, ALU.add, ALU.max))

            def find_row(v, rows, find, idx):
                below(rows, rows, v, find[1][:, :])
                chain(dve.tensor_scalar(find[1][:, :], find[1][:, :], -1.0, 0.0, ALU.add, ALU.max))
                chain(dve.scalar_tensor_tensor(out=find[0][:, :], in0=find[0][:, :], scalar=float(SLOTS // ROW),
                                               in1=find[1][:, :], op0=ALU.mult, op1=ALU.add))
                dve.tensor_copy(idx[:, :], find[0][:, :]).then_inc(find_ready, 1)

            def count_below(v, rows_i, near, find):
                chain(dve.tensor_scalar(rows_i, rows_i, SRC_BITS, None, ALU.logical_shift_right))
                below(near, rows_i, v, find[1][:, :])

            chain(dve.tensor_scalar(v_w[:, :], win_i[:, :], float(WIN), None, ALU.mult))
            chain(dve.tensor_copy(v_n[:, :], node_i[:, :]))
            dve.wait_ge(firsts_turned, 1)
            chain(dve.tensor_copy(firsts[:, :], ps_firsts))
            find_partition(v_w[:, :], near_w, find_w)
            dve.tensor_copy(idx_w[:, :], find_w[0][:, :]).then_inc(find_ready, 1)
            find_partition(v_n[:, :], near_n, find_n)
            dve.wait_ge(found[0], 16 * WIN_GROUPS)
            find_row(v_w[:, :], samples_w, find_w, idx_w)
            chain(dve.tensor_copy(ramp_f[:, :, :], ramp[:, :, :]))
            chain(dve.tensor_scalar(base_w[:, :], win_i[:, :], -float(CELLS), None, ALU.mult))
            dve.wait_ge(found[1], 16 * WIN_GROUPS)
            count_below(v_w[:, :], keys_w, near_w[:, :, 0:ROW], find_w)
            chain(dve.tensor_scalar(find_w[1][:, :], find_w[1][:, :], float(ROW), None, ALU.is_ge))
            chain(dve.tensor_tensor(find_w[0][:, :], find_w[0][:, :], find_w[1][:, :], ALU.add))
            dve.tensor_tensor(rows_w[:, :, :], ramp_f[:, :, :],
                              find_w[0][:, :].unsqueeze(2).to_broadcast([WIN_GROUP, WIN_GROUPS, WIN_ROWS]), ALU.add
                              ).then_inc(rows_ready, 1)
            dve.tensor_copy(idx_n[:, :], find_n[0][:, :]).then_inc(find_ready, 1)

            chain(dve.tensor_tensor(keep[:, 1:SLOTS], dst_f[:, 1:SLOTS], dst_f[:, 0:SLOTS - 1], ALU.is_equal))
            chain(dve.tensor_copy(start_f, start_i[:, :]))
            chain(dve.tensor_scalar(valid, start_f, float(LAST_N * SLOTS), None, ALU.is_lt))
            chain(dve.tensor_copy(prev_f, prev_i[:, :]))
            chain(dve.tensor_tensor(join, dst_f[:, 0:1], prev_f, ALU.is_equal))
            chain(dve.tensor_tensor(full, dst_f[:, 0:1], dst_f[:, SLOTS - 1:SLOTS], ALU.is_equal))
            chain(dve.tensor_tensor(cross, join, full, ALU.mult))
            chain(dve.tensor_scalar(scratch, dst_f[:, :], dst_f[:, 0:1], None, ALU.is_equal, ALU.add,
                                    accum_out=first_n))
            chain(dve.tensor_tensor(first_f, start_f, first_n, ALU.add))
            chain(dve.tensor_scalar(first_f, first_f, -1.0, None, ALU.add))
            chain(dve.tensor_copy(first_i[:, :], first_f))
            chain(dve.tensor_copy(picked_f.rearrange("p v c -> p (v c)"), src[:, PICK - 1:SLOTS:PICK]))
            dve.tensor_copy(wide[:, :], cross.to_broadcast([P, D])).then_inc(wide_ready, 1)
            dve.wait_ge(wideT_ready, 1)
            dve.tensor_copy(picked_i, ps_pickedT)
            dve.tensor_copy(crossT[:, :], ps_lastT).then_inc(crossT_copied, 1)

            def decode(g):
                par = g % 2
                d, t = win_tmp[:, 0, :], win_tmp[:, 1, :]
                dve.wait_ge(win_gathered[par], 16 * WIN_ROWS * (g // 2 + 1))
                key = win_keys[:, par, :]
                chain(dve.tensor_scalar(d, key, SRC_BITS, None, ALU.logical_shift_right))
                chain(dve.tensor_scalar(t, key, 7, 63, ALU.logical_shift_right, ALU.bitwise_and))
                if g >= 2:
                    dve.wait_ge(dec_turned, g - 1)
                chain(dve.scalar_tensor_tensor(out=decoded[:, par, 0, :], in0=d, scalar=float(TILES), in1=t,
                                               op0=ALU.mult, op1=ALU.add))
                chain(dve.tensor_scalar(decoded[:, par, 0, :], decoded[:, par, 0, :], base_w[:, g:g + 1], None,
                                        ALU.add))
                chain(dve.tensor_scalar(need_w[:, g:g + 1], decoded[:, par, 0, WIN_TILES * P - 1:WIN_TILES * P],
                                        float(CELLS), None, ALU.is_lt))
                chain(dve.tensor_scalar(d, key, P - 1, None, ALU.bitwise_and))
                dve.tensor_copy(decoded[:, par, 1, :], d).then_inc(decoded_ready, 1)
                dve.wait_ge(decoded_ready, g + 1)

            def one_hot(to, v, c):
                n = to.shape[2]
                shape = [P, HOT_ROWS, n // 2, 2]
                return dve.tensor_tensor(
                    to.rearrange("p m (n t) -> p m n t", t=2),
                    iota_c[:, 0:n].rearrange("p (n t) -> p n t", t=2).unsqueeze(1).to_broadcast(shape),
                    cols[:, v, c * HOT_ROWS:(c + 1) * HOT_ROWS, :].unsqueeze(2).to_broadcast(shape), ALU.is_equal)

            decode(0)
            for g in range(WIN_GROUPS):
                if g + 1 < WIN_GROUPS:
                    decode(g + 1)
                dve.wait_ge(colsT_ready, 2 * g + 2)
                with dve.Fori(g * WIN_BLOCKS, (g + 1) * WIN_BLOCKS) as r:
                    chain.enter(r, 1, g * WIN_BLOCKS)
                    dve.wait_ge(build_hot, r * 4 + 1)
                    n = cols.shape[2]
                    chain(dve.tensor_scalar(
                        cols[:, :, :, :],
                        colsT.rearrange("p v q j w -> p v (q j w)")[:, :, bass.ds(r * n, n)].unsqueeze(3)
                        .to_broadcast([P, 2, n, 2]), -1.0, float(CELLS), ALU.max, ALU.min))
                    for c in range(4):
                        dve.wait_ge(cells_ready, r * 4 + c + 1)
                        one_hot(cell_hot[:, c % 2, :, :], 0, c)
                        one_hot(low_hot[:, c % 2, :, :], 1, c).then_inc(build_hot, 1)
                    chain.leave(WIN_BLOCKS)
                if g == 4:
                    dve.wait_ge(found[2], 16 * TILES)
                    find_row(v_n[:, :], samples_n, find_n, idx_n)
                if g == 5:
                    dve.wait_ge(found[3], 16 * TILES)
                    count_below(v_n[:, :], keys_n, samples_n[:, :, 0:ROW], find_n)
                    dve.scalar_tensor_tensor(out=find_n[1][:, :], in0=find_n[0][:, :], scalar=float(ROW),
                                             in1=find_n[1][:, :], op0=ALU.mult, op1=ALU.add).then_inc(starts_made, 1)
                    dve.wait_ge(starts_made, 1)
                    dve.wait_ge(picked_stored, 16)
                    dve.memset(x[:, LAST, :], 0.0).then_inc(nodes_found, 1)
                    chain(dve.tensor_scalar(find_n[0][:, :], find_n[1][:, :], -1.0, 0.0, ALU.add, ALU.max))
                    chain(dve.tensor_copy(end_i[:, :], find_n[0][:, :]))
            dve.wait_ge(starts_loaded, 16)
            chain(dve.tensor_tensor(count[:, :], find_n[1][:, :], start_n[:, :], ALU.subtract))
            chain(dve.tensor_scalar(some[:, :], count[:, :], 0.0, None, ALU.is_gt))
            chain(dve.tensor_scalar(mean_scale[:, :], count[:, :], 1.0, None, ALU.max))
            chain(dve.reciprocal(mean_scale[:, :], mean_scale[:, :]))
            chain(dve.tensor_tensor(mean_scale[:, :], mean_scale[:, :], some[:, :], ALU.mult))
            dve.wait_ge(loaded, 16 * LOADS)
            dve.wait_ge(x_loaded, 32)
            dve.wait_ge(cells_copied, 4 * TILES + 2)
            dve.wait_ge(block_stored, 16 * TILES)
            chain(dve.tensor_reduce(bad[0:WIN_GROUP, 0:1], need_w[:, :], AX.X, ALU.max))
            chain(dve.tensor_reduce(bad[:, 1:2], over[:, :], AX.X, ALU.max))
            dve.tensor_tensor(bad[:, 0:1], bad[:, 0:1], bad[:, 1:2], ALU.max).then_inc(bad_ready, 1)
            dve.wait_ge(bad_summed, 1)
            dve.tensor_scalar(ok_i[:, :], ps_bad, 0.0, None, ALU.is_equal).then_inc(ok_ready, 1)
            dve.wait_ge(ok_ready, 1)
            dense = dve.value_load(ok_i[0:1, 0:1], min_val=0, max_val=1)
            end_stage(dve.tensor_copy(col[:, 7:8], col[:, 7:8]), 0)

            masks = [keep[:, :], crossT[:, :], join]

            def dense_pass(n, scale):
                step = dense_chain
                with dve.Fori(0, GROUPS) as r:
                    step.enter(r, GROUP)
                    for b in range(GROUP):
                        buf = b % A_BUFS
                        uses = len(range(buf, GROUP, A_BUFS))
                        dve.wait_ge(a_used[buf], r * uses + uses * GROUPS * n + b // A_BUFS + 2)
                        dve.wait_ge(acc_used, r * GROUP + TILES * n + b + GROUP)
                        step(dve.tensor_reduce(part_sum[:, b % 2, :],
                                               ps[:, b, 0:PARTS * D].rearrange("p (k f) -> p f k", k=PARTS),
                                               AX.X, ALU.add))
                        dve.tensor_scalar(agg[:, bass.ds(r * GROUP + b, 1), :].rearrange("p t f -> p (t f)"),
                                          part_sum[:, b % 2, :], scale[:, bass.ds(r * GROUP + b, 1)], None, ALU.mult
                                          ).then_inc(acc_used, 1)
                    step.leave(GROUPS)
                dve.wait_ge(acc_used, TILES * (n + 1) + GROUP)

            def take_group(q, n, g, scale, step):
                dve.wait_ge(q["agg_gathered"][g], 16 * GROUP * (n + 1))
                at = (slice(None), slice(g * GROUP, (g + 1) * GROUP), slice(None))
                step(dve.tensor_tensor(agg[at], agg[at], scale[:, at[1]].unsqueeze(2).to_broadcast([P, GROUP, D]),
                                       ALU.mult))

            def edge_pass(how, n, scale):
                q, step = sets[how], gather_chain[how]
                op0, op1 = (ALU.mult, ALU.add) if how == "sum" else (ALU.min, ALU.max)
                slots = [HALF - len(taken) if how == "max" else HALF for taken in PICKED]

                def make_hot(p, hf):
                    shape = [P, TILES, P // 2, 2]
                    dve.tensor_tensor(
                        hot[:, p, :, :].rearrange("p t (n c) -> p t n c", c=2),
                        pick_row[:, hf, p * P:(p + 1) * P].rearrange("p (n c) -> p n c", c=2)
                        .unsqueeze(1).to_broadcast(shape),
                        node_code[:, :, :].unsqueeze(2).to_broadcast(shape), ALU.is_equal).then_inc(hot_ready[p], 1)

                step(dve.memset(run[:, 1, HALF - 1, :], 0.0))
                for hf in range(2):
                    dve.tensor_copy(idx_stage[:, hf, :], src[:, hf * HALF:(hf + 1) * HALF]
                                    ).then_inc(q["idx_ready"][hf], 1)
                if how == "max":
                    dve.wait_ge(q["table_stored"], 16 * (n + 1))
                    for v, to in ((agg[:, 0:SPLIT, :], pick_parts[0]), (agg[:, SPLIT:TILES, :], pick_parts[1])):
                        step(dve.tensor_copy(to[:, :, 0, :], v))
                        step(dve.tensor_tensor(v, v, to[:, :, 0, :], ALU.subtract))
                        step(dve.tensor_copy(to[:, :, 1, :], v))
                        step(dve.tensor_tensor(to[:, :, 2, :], v, to[:, :, 1, :], ALU.subtract))
                    dve.wait_ge(pick_loaded[0], 16 * ((STEPS + 1) * n + 1))
                    for p in reversed(range(HALF_PICKS)):
                        make_hot(p, 0)
                with dve.Fori(0, STEPS) as r:
                    step.enter(r, 2 * HALF)
                    for hf in range(2):
                        if how == "max":
                            if hf == 0:
                                dve.wait_ge(pick_loaded[1], r * 16 + 16 * (STEPS * n + 1))
                            else:
                                dve.wait_ge(pick_loaded[0], r * 16 + 16 * ((STEPS + 1) * n + 2))
                                for p in range(1, HALF_PICKS):
                                    make_hot(p, 0)
                            for p in range(len(PICKED[hf])):
                                uses = PICK_HALVES[p]
                                dve.wait_ge(pick_ready[p], r * uses + uses * STEPS * n + hf + 1)
                                if p == 0:
                                    make_hot(p, 1 - hf)
                                dve.tensor_reduce(msg[:, hf, PICKED[hf][p], :],
                                                  ps_pick[p].rearrange("p (k f) -> p f k", k=PARTS),
                                                  AX.X, ALU.add).then_inc(pick_read[p], 1)
                        step(dve.tensor_copy(keep_stage[:, hf, :],
                                             keep[:, bass.ds(r * STEP + hf * HALF, HALF)]))
                        dve.wait_ge(q["gathered"][n][hf], r * (16 * slots[hf]) + 16 * slots[hf])
                        dve.tensor_copy(idx_stage[:, hf, :], src[:, bass.ds(r * STEP + STEP + hf * HALF, HALF)]
                                        ).then_inc(q["idx_ready"][hf], 1)
                        if how == "max":
                            dve.wait_ge(edge_ready[hf], r + STEPS * n + 2)
                            v = msg[:, hf, :, :].rearrange("p (g q) f -> p g (q f)", q=QUAD)
                            dve.tensor_tensor(v, v, ps_edge, ALU.add).then_inc(edge_used, 1)
                            dve.wait_ge(edge_used, r * 2 + 2 * STEPS * n + hf + 2)
                        dve.wait_ge(q["stored"][hf], r * 16 + 16 * STEPS * n + 16)
                        prev = run[:, 1 - hf, HALF - 1, :]
                        for s in range(HALF):
                            last = dve.scalar_tensor_tensor(
                                out=run[:, hf, s, :], in0=prev, scalar=keep_stage[:, hf, s:s + 1],
                                in1=msg[:, hf, s, :], op0=op0, op1=op1)
                            prev = run[:, hf, s, :]
                            if s < HALF - 1:
                                step(last)
                        last.then_inc(q["scanned"][hf], 1)
                        dve.wait_ge(q["scanned"][hf], r + STEPS * n + 2)
                    step.leave(STEPS)
                dve.wait_ge(q["lastT_ready"], n + 1)
                dve.tensor_tensor_scan(chainT[:, 1:P + 1], crossT[:, :], ps_lastT, 0.0, op0, op1
                                       ).then_inc(q["chain_ready"], 1)
                dve.wait_ge(q["carry_ready"], n + 1)
                dve.wait_ge(q["row_gathered"], 16 * (n + 1))
                dve.scalar_tensor_tensor(out=fixed[:, :], in0=ps_carry, scalar=join, in1=fix_row[:, :],
                                         op0=op0, op1=op1).then_inc(q["row_fixed"], 1)
                if how == "sum":
                    for g in range(GROUPS):
                        take_group(q, n, g, scale, step)

            def split(v, w, at):
                chain(dve.tensor_copy(parts[:, at[1], 0, :], v[at]))
                chain(dve.tensor_tensor(w[at], v[at], parts[:, at[1], 0, :], ALU.subtract))
                chain(dve.tensor_copy(parts[:, at[1], 1, :], w[at]))
                chain(dve.tensor_tensor(parts[:, at[1], 2, :], w[at], parts[:, at[1], 1, :], ALU.subtract))

            STEPS_OF = {"": 0, "norm": 7, "parts": 4, "norm parts": 11}

            def go_on(then, to, r, before):
                at = (slice(None), bass.ds(r * GROUP, GROUP), slice(None))
                shape = [P, GROUP, D]
                if "norm" in then:
                    m, v = group_mean[:, :], group_var[:, :]
                    dve.sem_inc(marks, 1)
                    chain(dve.tensor_reduce(m, x[at], AX.X, ALU.add))
                    chain(dve.tensor_scalar(m, m, -1.0 / D, None, ALU.mult))
                    chain(dve.tensor_tensor(tmp[at], x[at], m.unsqueeze(2).to_broadcast(shape), ALU.add))
                    chain(dve.tensor_tensor(h[at], tmp[at], tmp[at], ALU.mult))
                    dve.sem_inc(marks, 1)
                    chain(dve.tensor_reduce(v, h[at], AX.X, ALU.add))
                    dve.tensor_scalar(v, v, 1.0 / D, EPS, ALU.mult, ALU.add).then_inc(std_in, 1)
                    dve.wait_ge(std_out, r + before + 1)
                    chain(dve.reciprocal(v, v))
                    chain(dve.scalar_tensor_tensor(out=h[at], in0=tmp[at], scalar=0.0,
                                                   in1=v.unsqueeze(2).to_broadcast(shape),
                                                   op0=ALU.max, op1=ALU.mult))
                    to = h
                if "parts" in then:
                    split(to, tmp, at)

            def combine(what, g):
                n, base, how = what
                at = (slice(None), slice(g * GROUP, (g + 1) * GROUP), slice(None))
                base = node_tile[base]
                take_group(sets["max"], n, g, some, chain)
                chain(dve.tensor_tensor(tmp[at], agg[at], base[at], ALU.add))
                c = base if how == "leaky" else tmp
                last = dve.scalar_tensor_tensor(out=c[at], in0=tmp[at], scalar=0.01, in1=tmp[at],
                                                op0=ALU.mult, op1=ALU.max)
                if how == "leaky":
                    last.then_inc(combined, 1)
                else:
                    chain(last)
                    chain(dve.tensor_tensor(x[at], x[at], tmp[at], ALU.add))

            roots = sums = 0
            for i, k, stage in numbered():
                if stage[0] == "norm":
                    with dve.Fori(0, GROUPS) as r:
                        chain.enter(r, STEPS_OF[stage[1]])
                        go_on(stage[1], h, r, roots)
                        chain.leave(GROUPS)
                    roots += GROUPS
                    end_stage(dve.tensor_copy(col[:, 7:8], col[:, 7:8]), i)

                elif stage[0] == "combine":
                    dve.wait_ge(root_copied, STEPS * (stage[1][0] + 1))
                    for g in range(GROUPS):
                        combine(stage[1], g)
                        go_on(stage[2], h, g, roots)
                    roots += GROUPS
                    end_stage(dve.tensor_copy(col[:, 7:8], col[:, 7:8]), i)

                elif stage[0] == "project":
                    _, _, how, to, then, what = stage
                    to = node_tile[to]

                    def take_product(r):
                        at = (slice(None), bass.ds(r * GROUP, GROUP), slice(None))
                        dve.wait_ge(projected, r + GROUPS * k + 2)
                        if how == "relu":
                            last = dve.tensor_scalar(to[at], ps_out, 0.0, None, ALU.max)
                        elif how == "add":
                            last = dve.tensor_tensor(to[at], to[at], ps_out, ALU.add)
                        else:
                            last = dve.tensor_copy(to[at], ps_out)
                        last.then_inc(drained, 1)
                        if then:
                            dve.wait_ge(drained, r + GROUPS * k + 2)
                            go_on(then, to, r, roots)

                    if what:
                        dve.wait_ge(root_copied, STEPS * (what[0] + 1))
                        combine(what, 0)
                        for g in range(GROUPS):
                            if g + 1 < GROUPS:
                                combine(what, g + 1)
                            take_product(g)
                    else:
                        with dve.Fori(0, GROUPS) as r:
                            chain.enter(r, STEPS_OF[then])
                            take_product(r)
                            chain.leave(GROUPS)
                    if "norm" in then:
                        roots += GROUPS
                    dve.wait_ge(drained, GROUPS * (k + 1) + 1)
                    end_stage(dve.tensor_copy(col[:, 7:8], col[:, 7:8]), i)

                elif stage[0] == "graphnorm":
                    _, which, identity, to = stage
                    w, b, scale = (norm_p[:, 3 * which + j, :] for j in range(3))

                    def mask_pads():
                        chain(dve.tensor_scalar(tmp[:, LAST, :], tmp[:, LAST, :], valid, None, ALU.mult))

                    def sum_nodes(v):
                        dve.tensor_reduce(g_sum[:, :], v[:, :, :].rearrange("p t f -> p f t"), AX.X,
                                          ALU.add).then_inc(sum_in, 1)

                    mask_pads()
                    sum_nodes(tmp)
                    sums += 1
                    dve.wait_ge(sum_out, sums)
                    chain(dve.tensor_scalar(g_a[:, :], ps_stat, -1.0 / N, None, ALU.mult))
                    chain(dve.tensor_tensor(g_a[:, :], g_a[:, :], scale, ALU.mult))
                    chain(dve.tensor_tensor(tmp[:, :, :], tmp[:, :, :], over_tiles(g_a[:, :]), ALU.add))
                    mask_pads()
                    chain(dve.tensor_tensor(agg[:, :, :], tmp[:, :, :], tmp[:, :, :], ALU.mult))
                    sum_nodes(agg)
                    sums += 1
                    dve.wait_ge(sum_out, sums)
                    roots += 1
                    dve.tensor_scalar(g_b[:, :], ps_stat, 1.0 / N, EPS, ALU.mult, ALU.add).then_inc(std_in, 1)
                    dve.wait_ge(std_out, roots)
                    chain(dve.reciprocal(g_b[:, :], g_b[:, :]))
                    chain(dve.tensor_tensor(g_b[:, :], g_b[:, :], w, ALU.mult))
                    chain(dve.tensor_tensor(tmp[:, :, :], tmp[:, :, :], over_tiles(g_b[:, :]), ALU.mult))
                    chain(dve.tensor_tensor(tmp[:, :, :], tmp[:, :, :], over_tiles(b), ALU.add))
                    last = dve.scalar_tensor_tensor(
                        out=h2[:, :, :], in0=tmp[:, :, :], scalar=0.0,
                        in1=node_tile[identity][:, :, :], op0=ALU.max, op1=ALU.add)
                    if to == "x":
                        chain(last)
                        last = dve.tensor_tensor(x[:, :, :], x[:, :, :], h2[:, :, :], ALU.add)
                    else:
                        chain(last)
                        split(h2, tmp, (slice(None),) * 3)
                        last = dve.tensor_copy(col[:, 7:8], col[:, 7:8])
                    end_stage(last, i)

                elif stage[0] == "edges":
                    how, n = place(k)
                    scale = {"mean": mean_scale, "some": some}[stage[3]]
                    if how == "sum":
                        with dve.If(dense):
                            dense_pass(n, scale)
                        with dve.Else():
                            edge_pass(how, n, scale)
                    else:
                        if n == 0:
                            for v in masks:
                                chain(dve.tensor_scalar(v, v, 2.0, -1.0, ALU.mult, ALU.add))
                                chain(dve.tensor_scalar(v, v, BIG, None, ALU.mult))
                        edge_pass(how, n, scale)
                        if n == 1:
                            for v in masks:
                                chain(dve.tensor_scalar(v, v, 0.0, None, ALU.is_gt))
                    end_stage(dve.tensor_copy(col[:, 7:8], col[:, 7:8]), i)


_INS = ["x", "src", "dst", "edge_attr_32", "L2_gnn_W1_edge", "L2_gnn_W2_edge"] + WEIGHTS + list(BIASES.values()) + NORMS


def kernel(**inputs):
    import numpy as np
    import concourse.bacc as bacc
    from concourse.bass_utils import run_bass_kernel_spmd

    nc = bacc.Bacc("TRN2", target_bir_lowering=False, num_devices=1)
    arrays, aps = {}, {}
    for name in _INS:
        v = np.ascontiguousarray(inputs[name])
        arrays[f"in_{name}"] = v
        aps[name] = nc.dram_tensor(f"in_{name}", v.shape, mybir.dt.from_np(v.dtype), kind="ExternalInput").ap()
    out = nc.dram_tensor("out", (N, D), mybir.dt.float32, kind="ExternalOutput").ap()
    build(nc, aps, out)
    r = run_bass_kernel_spmd(nc, [arrays], core_ids=[0])
    return r.results[0]["out"]
```
